# Optimizing a Trainium2 kernel written in Bass

```python
import numpy as np
import jax
import jax.numpy as jnp

def _softmax(x, axis=-1):
    return jax.nn.softmax(x, axis=axis)

def _gelu(x):
    return jax.nn.gelu(x, approximate=True)

def _silu(x):
    return jax.nn.silu(x)

def _sigmoid(x):
    return jax.nn.sigmoid(x)

def _layernorm(x, axis=-1, eps=1e-05):
    m = jnp.mean(x, axis=axis, keepdims=True)
    v = jnp.var(x, axis=axis, keepdims=True)
    return (x - m) / jnp.sqrt(v + eps)

def _scatter_add(tgt, idx, src, axis=0):
    return tgt.at[idx].add(src)

def _segment_sum(src, seg, n):
    return jax.ops.segment_sum(src, seg, n)
kernel_name = 'mk_dlrm_tower_d1_rec_r8_151c11'

def setup_inputs(seed: int=0):
    np.random.seed(seed)
    _w = jnp.asarray

    def _rec_inputs():
        import jax
        import jax.numpy as jnp
        _tk = jax.random.key(seed)
        ids = jnp.stack([jax.random.randint(jax.random.fold_in(_tk, 200 + f), (512,), 0, v, jnp.int32) for f, v in enumerate([12500, 1000, 12500, 1000, 1000, 125000, 125000, 12500, 125000, 12500, 1000, 1250, 1000, 12500, 1250, 1000, 12500, 1000, 1250, 1000, 1000, 1000, 1000, 12500, 12500, 1000])], axis=1)
        tbl_0 = 0.05 * jax.random.normal(jax.random.fold_in(_tk, 500 + 0), (12500, 64), jnp.float32)
        tbl_1 = 0.05 * jax.random.normal(jax.random.fold_in(_tk, 500 + 1), (1000, 64), jnp.float32)
        tbl_2 = 0.05 * jax.random.normal(jax.random.fold_in(_tk, 500 + 2), (12500, 64), jnp.float32)
        tbl_3 = 0.05 * jax.random.normal(jax.random.fold_in(_tk, 500 + 3), (1000, 64), jnp.float32)
        tbl_4 = 0.05 * jax.random.normal(jax.random.fold_in(_tk, 500 + 4), (1000, 64), jnp.float32)
        tbl_5 = 0.05 * jax.random.normal(jax.random.fold_in(_tk, 500 + 5), (125000, 64), jnp.float32)
        tbl_6 = 0.05 * jax.random.normal(jax.random.fold_in(_tk, 500 + 6), (125000, 64), jnp.float32)
        tbl_7 = 0.05 * jax.random.normal(jax.random.fold_in(_tk, 500 + 7), (12500, 64), jnp.float32)
        tbl_8 = 0.05 * jax.random.normal(jax.random.fold_in(_tk, 500 + 8), (125000, 64), jnp.float32)
        tbl_9 = 0.05 * jax.random.normal(jax.random.fold_in(_tk, 500 + 9), (12500, 64), jnp.float32)
        tbl_10 = 0.05 * jax.random.normal(jax.random.fold_in(_tk, 500 + 10), (1000, 64), jnp.float32)
        tbl_11 = 0.05 * jax.random.normal(jax.random.fold_in(_tk, 500 + 11), (1250, 64), jnp.float32)
        tbl_12 = 0.05 * jax.random.normal(jax.random.fold_in(_tk, 500 + 12), (1000, 64), jnp.float32)
        tbl_13 = 0.05 * jax.random.normal(jax.random.fold_in(_tk, 500 + 13), (12500, 64), jnp.float32)
        tbl_14 = 0.05 * jax.random.normal(jax.random.fold_in(_tk, 500 + 14), (1250, 64), jnp.float32)
        tbl_15 = 0.05 * jax.random.normal(jax.random.fold_in(_tk, 500 + 15), (1000, 64), jnp.float32)
        tbl_16 = 0.05 * jax.random.normal(jax.random.fold_in(_tk, 500 + 16), (12500, 64), jnp.float32)
        tbl_17 = 0.05 * jax.random.normal(jax.random.fold_in(_tk, 500 + 17), (1000, 64), jnp.float32)
        tbl_18 = 0.05 * jax.random.normal(jax.random.fold_in(_tk, 500 + 18), (1250, 64), jnp.float32)
        tbl_19 = 0.05 * jax.random.normal(jax.random.fold_in(_tk, 500 + 19), (1000, 64), jnp.float32)
        tbl_20 = 0.05 * jax.random.normal(jax.random.fold_in(_tk, 500 + 20), (1000, 64), jnp.float32)
        tbl_21 = 0.05 * jax.random.normal(jax.random.fold_in(_tk, 500 + 21), (1000, 64), jnp.float32)
        tbl_22 = 0.05 * jax.random.normal(jax.random.fold_in(_tk, 500 + 22), (1000, 64), jnp.float32)
        tbl_23 = 0.05 * jax.random.normal(jax.random.fold_in(_tk, 500 + 23), (12500, 64), jnp.float32)
        tbl_24 = 0.05 * jax.random.normal(jax.random.fold_in(_tk, 500 + 24), (12500, 64), jnp.float32)
        tbl_25 = 0.05 * jax.random.normal(jax.random.fold_in(_tk, 500 + 25), (1000, 64), jnp.float32)
        _rk = jax.random.fold_in(_tk, 7)
        r_dense_t = 7.22013e-05 + 1.00017 * jax.random.normal(jax.random.fold_in(_rk, 101), (512, 256), jnp.float32)
        W_top1 = 0.0360844 * jax.random.normal(jax.random.fold_in(_tk, 801), (768, 512), jnp.float32)
        W_top2 = 0.0441942 * jax.random.normal(jax.random.fold_in(_tk, 802), (512, 256), jnp.float32)
        W_top3 = 0.0625 * jax.random.normal(jax.random.fold_in(_tk, 803), (256, 1), jnp.float32)
        b_top1 = jnp.zeros((512,), jnp.float32)
        b_top2 = jnp.zeros((256,), jnp.float32)
        return (r_dense_t, ids, tbl_0, tbl_1, tbl_2, tbl_3, tbl_4, tbl_5, tbl_6, tbl_7, tbl_8, tbl_9, tbl_10, tbl_11, tbl_12, tbl_13, tbl_14, tbl_15, tbl_16, tbl_17, tbl_18, tbl_19, tbl_20, tbl_21, tbl_22, tbl_23, tbl_24, tbl_25, W_top1, b_top1, W_top2, b_top2, W_top3)
    r_dense_t, ids, tbl_0, tbl_1, tbl_2, tbl_3, tbl_4, tbl_5, tbl_6, tbl_7, tbl_8, tbl_9, tbl_10, tbl_11, tbl_12, tbl_13, tbl_14, tbl_15, tbl_16, tbl_17, tbl_18, tbl_19, tbl_20, tbl_21, tbl_22, tbl_23, tbl_24, tbl_25, W_top1, b_top1, W_top2, b_top2, W_top3 = _rec_inputs()

    def _L0_rec_setup():
        import jax, jax.numpy as jnp
        import numpy as np
        EPS = 1e-05
        NI = 33
        TRIL_I, TRIL_J = np.tril_indices(NI, k=-1)

        def layer_norm(x, g, b):
            m = jnp.mean(x, axis=-1, keepdims=True)
            v = jnp.mean(jnp.square(x - m), axis=-1, keepdims=True)
            return (x - m) * jax.lax.rsqrt(v + EPS) * g + b
        key = jax.random.key(seed)
        ks = jax.random.split(key, 8)
        B, D_DENSE, N_SP, D_SP = (4096, 256, 26, 64)
        E, PROJ, MAXD, NFLAT = (128, 32, 512, 528)
        dense_t = jax.random.normal(ks[0], (B, D_DENSE), dtype=jnp.float32)
        sparse_t = jax.random.normal(ks[1], (B, N_SP, D_SP), dtype=jnp.float32)
        Wd = jax.random.normal(ks[2], (E, D_DENSE), dtype=jnp.float32) / np.sqrt(D_DENSE)
        Ws = jax.random.normal(ks[3], (E, D_SP), dtype=jnp.float32) / np.sqrt(D_SP)
        Wsi = jax.random.normal(ks[4], (PROJ, N_SP), dtype=jnp.float32) / np.sqrt(N_SP)
        Wl = jax.random.normal(ks[5], (MAXD, NFLAT), dtype=jnp.float32) / np.sqrt(NFLAT)
        gd = jnp.ones((E,), jnp.float32)
        bd = jnp.zeros((E,), jnp.float32)
        gs = jnp.ones((E,), jnp.float32)
        bs = jnp.zeros((E,), jnp.float32)
        gsi = jnp.ones((PROJ,), jnp.float32)
        bsi = jnp.zeros((PROJ,), jnp.float32)
        gl = jnp.ones((MAXD,), jnp.float32)
        bl = jnp.zeros((MAXD,), jnp.float32)
        return {'dense_t': dense_t, 'sparse_t': sparse_t, 'Wd': Wd, 'gd': gd, 'bd': bd, 'Ws': Ws, 'gs': gs, 'bs': bs, 'Wsi': Wsi, 'gsi': gsi, 'bsi': bsi, 'Wl': Wl, 'gl': gl, 'bl': bl, 'dims_in_use': 384}
    _L0_rec_all = _L0_rec_setup()
    _L0_rec_in = {k: v for k, v in _L0_rec_all.items() if k in ('Wd', 'gd', 'bd', 'Ws', 'gs', 'bs', 'Wsi', 'gsi', 'bsi', 'Wl', 'gl', 'bl')}
    del _L0_rec_all
    return {'r_dense_t': r_dense_t, 'ids': ids, 'tbl_0': tbl_0, 'tbl_1': tbl_1, 'tbl_2': tbl_2, 'tbl_3': tbl_3, 'tbl_4': tbl_4, 'tbl_5': tbl_5, 'tbl_6': tbl_6, 'tbl_7': tbl_7, 'tbl_8': tbl_8, 'tbl_9': tbl_9, 'tbl_10': tbl_10, 'tbl_11': tbl_11, 'tbl_12': tbl_12, 'tbl_13': tbl_13, 'tbl_14': tbl_14, 'tbl_15': tbl_15, 'tbl_16': tbl_16, 'tbl_17': tbl_17, 'tbl_18': tbl_18, 'tbl_19': tbl_19, 'tbl_20': tbl_20, 'tbl_21': tbl_21, 'tbl_22': tbl_22, 'tbl_23': tbl_23, 'tbl_24': tbl_24, 'tbl_25': tbl_25, 'W_top1': W_top1, 'b_top1': b_top1, 'W_top2': W_top2, 'b_top2': b_top2, 'W_top3': W_top3, 'L0_rec_Wd': _L0_rec_in['Wd'], 'L0_rec_gd': _L0_rec_in['gd'], 'L0_rec_bd': _L0_rec_in['bd'], 'L0_rec_Ws': _L0_rec_in['Ws'], 'L0_rec_gs': _L0_rec_in['gs'], 'L0_rec_bs': _L0_rec_in['bs'], 'L0_rec_Wsi': _L0_rec_in['Wsi'], 'L0_rec_gsi': _L0_rec_in['gsi'], 'L0_rec_bsi': _L0_rec_in['bsi'], 'L0_rec_Wl': _L0_rec_in['Wl'], 'L0_rec_gl': _L0_rec_in['gl'], 'L0_rec_bl': _L0_rec_in['bl']}

def reference(r_dense_t, ids, tbl_0, tbl_1, tbl_2, tbl_3, tbl_4, tbl_5, tbl_6, tbl_7, tbl_8, tbl_9, tbl_10, tbl_11, tbl_12, tbl_13, tbl_14, tbl_15, tbl_16, tbl_17, tbl_18, tbl_19, tbl_20, tbl_21, tbl_22, tbl_23, tbl_24, tbl_25, W_top1, b_top1, W_top2, b_top2, W_top3, L0_rec_Wd, L0_rec_gd, L0_rec_bd, L0_rec_Ws, L0_rec_gs, L0_rec_bs, L0_rec_Wsi, L0_rec_gsi, L0_rec_bsi, L0_rec_Wl, L0_rec_gl, L0_rec_bl):
    import jax
    import jax.numpy as jnp

    def _L0_rec_ref(dense_t, sparse_t, Wd, gd, bd, Ws, gs, bs, Wsi, gsi, bsi, Wl, gl, bl, dims_in_use):
        import jax, jax.numpy as jnp
        import numpy as np
        EPS = 1e-05
        NI = 33
        TRIL_I, TRIL_J = np.tril_indices(NI, k=-1)

        def layer_norm(x, g, b):
            m = jnp.mean(x, axis=-1, keepdims=True)
            v = jnp.mean(jnp.square(x - m), axis=-1, keepdims=True)
            return (x - m) * jax.lax.rsqrt(v + EPS) * g + b
        x = layer_norm(dense_t @ Wd.T, gd, bd)
        y = layer_norm(jnp.einsum('bnd,ed->bne', sparse_t, Ws), gs, bs)
        y = jnp.einsum('bne,pn->bep', y, Wsi)
        y = layer_norm(y, gsi, bsi)
        y = jnp.swapaxes(y, 1, 2)
        T = jnp.concatenate([x[:, None, :], y], axis=1)
        Z = jnp.einsum('bnd,bmd->bnm', T, T)
        Zflat = Z[:, TRIL_I, TRIL_J]
        out = layer_norm(Zflat @ Wl.T, gl, bl)
        maxd = out.shape[-1]
        mask = (jnp.arange(maxd) < dims_in_use).astype(out.dtype)
        return out * mask
    e = jnp.stack([tbl_0[ids[:, 0]], tbl_1[ids[:, 1]], tbl_2[ids[:, 2]], tbl_3[ids[:, 3]], tbl_4[ids[:, 4]], tbl_5[ids[:, 5]], tbl_6[ids[:, 6]], tbl_7[ids[:, 7]], tbl_8[ids[:, 8]], tbl_9[ids[:, 9]], tbl_10[ids[:, 10]], tbl_11[ids[:, 11]], tbl_12[ids[:, 12]], tbl_13[ids[:, 13]], tbl_14[ids[:, 14]], tbl_15[ids[:, 15]], tbl_16[ids[:, 16]], tbl_17[ids[:, 17]], tbl_18[ids[:, 18]], tbl_19[ids[:, 19]], tbl_20[ids[:, 20]], tbl_21[ids[:, 21]], tbl_22[ids[:, 22]], tbl_23[ids[:, 23]], tbl_24[ids[:, 24]], tbl_25[ids[:, 25]]], axis=1)
    z = _L0_rec_ref(r_dense_t, e, L0_rec_Wd, L0_rec_gd, L0_rec_bd, L0_rec_Ws, L0_rec_gs, L0_rec_bs, L0_rec_Wsi, L0_rec_gsi, L0_rec_bsi, L0_rec_Wl, L0_rec_gl, L0_rec_bl, 384)
    z = z.reshape(z.shape[0], -1)
    h = jnp.concatenate([z, r_dense_t], axis=1)
    h = jnp.maximum(h @ W_top1 + b_top1, 0.0)
    h = jnp.maximum(h @ W_top2 + b_top2, 0.0)
    y = h @ W_top3
    return y

_drawn_inputs = setup_inputs


def setup_inputs(seed=0):
    import zlib

    import numpy as np

    out = dict(_drawn_inputs(seed))
    spreads = {'b_top1': (0.0, 0.1),
     'b_top2': (0.0, 0.1),
     'L0_rec_gd': (1.0, 0.6),
     'L0_rec_bd': (0.0, 0.8),
     'L0_rec_gs': (1.0, 0.6),
     'L0_rec_bs': (0.0, 0.1),
     'L0_rec_gsi': (1.0, 0.2),
     'L0_rec_bsi': (0.0, 0.1),
     'L0_rec_gl': (1.0, 0.2),
     'L0_rec_bl': (0.0, 0.1)}
    factors = {}
    for name, (base, spread) in spreads.items():
        noise = np.random.default_rng([zlib.crc32(name.encode()), seed]).standard_normal(out[name].shape)
        drawn = base * np.exp(spread * noise) if base else spread * noise
        out[name] = jnp.asarray(drawn.astype(out[name].dtype))
    for name, factor in factors.items():
        out[name] = (out[name] * factor).astype(out[name].dtype)
    return out
```

```python
from contextlib import ExitStack

import numpy as np
import concourse.bass as bass
from concourse import mybir

VOCAB = [12500, 1000, 12500, 1000, 1000, 125000, 125000, 12500, 125000, 12500, 1000, 1250, 1000,
         12500, 1250, 1000, 12500, 1000, 1250, 1000, 1000, 1000, 1000, 12500, 12500, 1000]
B, NF, D, E, PJ = 512, len(VOCAB), 64, 128, 32
DENSE, UO, USED, H1, H2 = 256, 512, 384, 512, 256
P = 128
NBLK = B // P
NC = NF
NPAIR = NC // 2
SBANK = 512 // PJ
NBANK = P // SBANK
NCOL = PJ + 2
QUADS = P // 4
ZQ = 8
NZ = QUADS // ZQ
QG = PJ // 4
TW = 13
SPAN = 6
EPS = 1e-5

COLS = [("bq", QG), ("gq", QG), ("bp", 1), ("gp", 1), ("gs", 1), ("bs", 1), ("gd", 1), ("bd", 1),
        ("gl", USED // P), ("bl", USED // P), ("b1", H1 // P), ("b2", H2 // P), ("w3", H2 // P)]


def chunk_samples(c):
    return (P * c) // NF, (P * c + P - 1) // NF


def last_chunk(m):
    return (SBANK * NF * (m + 1) - 1) // P


def first_chunk(m):
    return (SBANK * NF * m) // P


def build(nc, tables, index, consts, small, ws_t, wsi_rows, dense_t, wd_t, wl, wlx, w1, w2, out):
    F32, I32 = mybir.dt.float32, mybir.dt.int32
    ALU, ACT, AX = mybir.AluOpType, mybir.ActivationFunctionType, mybir.AxisListType

    with ExitStack() as ctx:
        def sb(name, shape, dt=F32):
            return ctx.enter_context(nc.sbuf_tensor(name, shape, dt))

        def sem(name):
            return ctx.enter_context(nc.semaphore(name))

        def bank(name):
            return ctx.enter_context(nc.psum_tensor(name, [P, 512], F32))

        idx_in = sb("idx_in", [P, 2, NBLK * NC], I32)
        idx = sb("idx", [P, NBLK * NC], I32)
        const = sb("const", [P, P + TW * SPAN + PJ])
        cols = sb("cols", [P, sum(w for _, w in COLS)])
        ws_sb = sb("ws_sb", [P, E])
        wsi_sb = sb("wsi_sb", [P, TW, PJ])
        dense_sb = sb("dense_sb", [P, DENSE // P, B])
        wd_sb = sb("wd_sb", [P, DENSE // P, E])
        wl_sb = sb("wl_sb", [P, QG, UO])
        wlx_sb = sb("wlx_sb", [PJ, UO])
        w1_sb = sb("w1_sb", [P, (USED + DENSE) // P, H1])
        w2_sb = sb("w2_sb", [P, H1 // P, H2])
        ident = const[:, 0:P]
        mask = const[:, P:P + TW * SPAN].rearrange("p (c k) -> p c k", k=SPAN)
        eye = const[:, P + TW * SPAN:P + TW * SPAN + PJ]
        col = {}
        n = 0
        for name, width in COLS:
            col[name] = cols[:, n:n + width]
            n += width

        eps = sb("eps", [P, 1])
        ones = sb("ones", [P, P])
        wsm = sb("wsm", [P, 2])
        wsc = sb("wsc", [P, 2 * E])
        wsim = sb("wsim", [P, 2, TW])
        wsic = sb("wsic", [P, TW, PJ])
        wexp = sb("wexp", [P, TW, SPAN, PJ])
        bias = sb("bias", [P, PJ])
        gg = sb("gg", [P, QG])
        wg = sb("wg", [P, QG, UO])
        beye = sb("beye", [P, QG, PJ])
        bp64 = sb("bp64", [P, 1])
        w9 = sb("w9", [P, UO])
        w9c = sb("w9c", [P, UO])
        wlm = sb("wlm", [P, 2, QG])
        w9m = sb("w9m", [P, 2])
        wbraw = sb("wbraw", [P, UO])
        xstat = sb("xstat", [P, NBLK, 6])
        xmv = sb("xmv", [P, NBLK, 2])
        xsd = sb("xsd", [P, NBLK])
        xrs = sb("xrs", [P, NBLK])
        xn = sb("xn", [P, NBLK, E])
        xT = sb("xT", [P, B])
        xsum = sb("xsum", [P, B])
        rows = sb("rows", [P, NPAIR, 2 * D])
        rowsT = sb("rowsT", [P, NPAIR, P])
        junk = sb("junk", [P, 2, E])
        yss = sb("yss", [P, NPAIR, 2])
        ysd = sb("ysd", [P, NPAIR, 2])
        yrs = sb("yrs", [P, NPAIR, 2])
        yn = sb("yn", [P, NPAIR, 2, E])
        t1 = sb("t1", [P, NBANK, SBANK, PJ])
        t2 = sb("t2", [P, NBANK, SBANK, PJ])
        tss = sb("tss", [P, NBANK, SBANK])
        tsd = sb("tsd", [P, NBANK, SBANK])
        trs = sb("trs", [P, NBANK, SBANK])
        T = sb("T", [P, P, NCOL])
        zs = sb("zs", [P, NCOL, QUADS])
        zr = sb("zr", [P, QG, P])
        z9 = sb("z9", [P, P])
        ujunk = sb("ujunk", [P, UO])
        uss = sb("uss", [P, 1])
        usd = sb("usd", [P, 1])
        urs = sb("urs", [P, 1])
        un = sb("un", [P, USED])
        znT = sb("znT", [P, USED // P, P])
        h1 = sb("h1", [P, H1 // P, P])
        h2 = sb("h2", [P, H2 // P, P])
        ysb = sb("ysb", [1, B])

        pR = bank("pR")
        pY = [bank("pY0"), bank("pY1")]
        pT = [bank("pT0"), bank("pT1")]
        pZ = [bank("pZ0"), bank("pZ1")]
        pU = bank("pU")

        ld_index, ld_const, ld_cols, ld_ws, ld_wsi = map(sem, ["ld_index", "ld_const", "ld_cols", "ld_ws", "ld_wsi"])
        ld_dense, ld_wd, ld_wl, ld_wlx, ld_w1, ld_w2 = map(
            sem, ["ld_dense", "ld_wd", "ld_wl", "ld_wlx", "ld_w1", "ld_w2"])
        idx_ready, fills_ready, wsc_ready, wexp_ready = map(sem, ["idx_ready", "fills_ready", "wsc_ready", "wexp_ready"])
        x_done, x_var, x_std, x_norm = map(sem, ["x_done", "x_var", "x_std", "x_norm"])
        xT_done, xT_sb, xsum_done, xsum_sb = map(sem, ["xT_done", "xT_sb", "xsum_done", "xsum_sb"])
        bias_done, bias_sb, beye_ready, wb_done, wb_sb, wrow_done, w_ready = map(
            sem, ["bias_done", "bias_sb", "beye_ready", "wb_done", "wb_sb", "wrow_done", "w_ready"])
        gathered = [sem(f"gathered{i}") for i in range(NPAIR)]
        r_done, r_sb, y_done, y_sq, y_std, y_rs, y_sb = map(
            sem, ["r_done", "r_sb", "y_done", "y_sq", "y_std", "y_rs", "y_sb"])
        t_done, t1_sb, t_sq, t_var, t_std, t_rs, t_sb, xcol_sb = map(
            sem, ["t_done", "t1_sb", "t_sq", "t_var", "t_std", "t_rs", "t_sb", "xcol_sb"])
        z_done, zs_sb, z9_sb, zr_sb = map(sem, ["z_done", "zs_sb", "z9_sb", "zr_sb"])
        u_done, u_sq, u_std, u_rs, u_sb = map(sem, ["u_done", "u_sq", "u_std", "u_rs", "u_sb"])
        zT_done, zT_sb, h1_done, h1_sb, h2_done, h2_sb, o_done, o_sb, out_done = map(
            sem, ["zT_done", "zT_sb", "h1_done", "h1_sb", "h2_done", "h2_sb", "o_done", "o_sb", "out_done"])
        setup = sem("setup")

        block = ctx.enter_context(nc.Block())

        bank_step = [last_chunk(m) // 2 + 3 for m in range(NBANK)]
        z_step = [bank_step[2 * h + 1] + 2 for h in range(NZ)]
        zr_step = z_step[-1] + 1
        u_step = zr_step + 1
        zT_step, h1_step, h2_step, o_step = u_step + 2, u_step + 3, u_step + 4, u_step + 5
        STEPS = o_step + 1

        def run(eng, step):
            for i in range(NPAIR):
                step((0, 0), i)
            with eng.Fori(0, NBLK - 1) as r:
                for i in range(NPAIR):
                    if i + NPAIR < STEPS:
                        step((r, 0), i + NPAIR)
                    step((r, 1), i)
            for i in range(NPAIR, STEPS):
                step((0, NBLK - 1), i)

        def count(k, per_block, n):
            return k[0] * per_block + (k[1] * per_block + n)

        def later(k):
            return not (isinstance(k[0], int) and k[0] + k[1] == 0)

        def samples(k):
            return bass.ds(k[0] * P + k[1] * P, P)

        @block.sync
        def _(sp):
            for dst, src, done in [(idx_in[:], index, ld_index), (ws_sb[:], ws_t, ld_ws), (const[:], consts, ld_const),
                                   (wsi_sb[:], wsi_rows, ld_wsi), (cols[:], small, ld_cols),
                                   (dense_sb[:], dense_t, ld_dense), (wd_sb[:], wd_t, ld_wd), (wlx_sb[:], wlx, ld_wlx),
                                   (wl_sb[:], wl, ld_wl), (w1_sb[:, 0:USED // P, :],
                                                           w1[0:USED, :].rearrange("(c p) n -> p c n", p=P), ld_w1),
                                   (w1_sb[:, USED // P:, :],
                                    w1[UO:UO + DENSE, :].rearrange("(c p) n -> p c n", p=P), ld_w1),
                                   (w2_sb[:], w2.rearrange("(c p) n -> p c n", p=P), ld_w2)]:
                sp.dma_start(dst, src).then_inc(done, 16)
            sp.wait_ge(o_sb, NBLK)
            sp.dma_start(out, ysb[:]).then_inc(out_done, 16)
            sp.wait_ge(out_done, 16)

        @block.gpsimd
        def _(pool):
            pool.wait_ge(idx_ready, 1)
            for k in range(NBLK):
                for c in range(NC):
                    if k and c % 2 == 0:
                        pool.wait_ge(r_done, NPAIR * (k - 1) + c // 2 + 1)
                    pool.indirect_dma_start(
                        out=rows[:, c // 2, (c % 2) * D:(c % 2 + 1) * D], out_offset=None, in_=tables,
                        in_offset=bass.IndirectOffsetOnAxis(ap=idx[:, NC * k + c:NC * k + c + 1], axis=0),
                    ).then_inc(gathered[c // 2], 16)

        @block.tensor
        def _(pe):
            mm = nc.tensor.matmul

            def step(k, i):
                if i < NPAIR:
                    pe.wait_ge(gathered[i], count(k, 32, 32))
                    if i or later(k):
                        pe.wait_ge(r_sb, count(k, NPAIR, i))
                    nc.tensor.transpose(pR[:, 0:P], rows[:, i, :], ident).then_inc(r_done, 1)
                j = i - 1
                if 0 <= j < NPAIR:
                    pe.wait_ge(r_sb, count(k, NPAIR, j + 1))
                    before = j - 2 if j >= 2 else (NPAIR - 1 if j == 0 else NPAIR - 2) - NPAIR
                    if before >= 0 or later(k):
                        pe.wait_ge(y_sb, count(k, NPAIR, before + 1))
                    mm(pY[j % 2][:, 0:2 * E], rowsT[:, j, :], wsc[:], start=True, stop=True).then_inc(y_done, 1)
                j = i - 3
                if 0 <= j < NPAIR:
                    pe.wait_ge(y_sb, count(k, NPAIR, j + 1))
                    for c in (2 * j, 2 * j + 1):
                        lo, hi = chunk_samples(c)
                        for m in range(lo // SBANK, hi // SBANK + 1):
                            a, z = max(lo, SBANK * m), min(hi, SBANK * (m + 1) - 1)
                            first = c == first_chunk(m)
                            if first and (m >= 2 or later(k)):
                                pe.wait_ge(t1_sb, count(k, NBANK, m - 1))
                            got = mm(pT[m % 2][:, PJ * (a - SBANK * m):PJ * (z + 1 - SBANK * m)], yn[:, j, c % 2, :],
                                     wexp[:, c % TW, a - lo:z + 1 - lo, :], start=first, stop=c == last_chunk(m),
                                     skip_group_check=True)
                            if c == last_chunk(m):
                                got.then_inc(t_done, 1)
                for h in range(NZ):
                    if i == z_step[h]:
                        pe.wait_ge(t_sb, count(k, NBANK, 2 * h + 2))
                        pe.wait_ge(xcol_sb, count(k, 2, h // 2 + 1))
                        if h >= 2 or later(k):
                            pe.wait_ge(zs_sb, count(k, NZ, h - 1))
                        for g in range(ZQ):
                            for s in range(4):
                                t = 4 * (ZQ * h + g) + s
                                got = mm(pZ[h % 2][32 * s:32 * s + 32, NCOL * g:NCOL * (g + 1)], T[:, t, 0:PJ],
                                         T[:, t, :], start=True, stop=True)
                        got.then_inc(z_done, 1)
                if i == u_step:
                    pe.wait_ge(zr_sb, count(k, 1, 1))
                    pe.wait_ge(z9_sb, count(k, 1, 1))
                    if later(k):
                        pe.wait_ge(o_sb, count(k, 1, 0))
                    for q in range(QG):
                        mm(pU[:], zr[:, q, :], wg[:, q, :], start=q == 0, stop=False)
                    mm(pU[:], z9[:], w9c[:], start=False, stop=True).then_inc(u_done, 1)
                if i == zT_step:
                    pe.wait_ge(u_sb, count(k, 1, 1))
                    for c in range(USED // P):
                        got = nc.tensor.transpose(pU[:, P * c:P * (c + 1)], un[:, P * c:P * (c + 1)], ident)
                    got.then_inc(zT_done, 1)
                if i == h1_step:
                    pe.wait_ge(zT_sb, count(k, 1, 1))
                    NK = (USED + DENSE) // P
                    for m in range(H1 // P):
                        for c in range(NK):
                            rhs = znT[:, c, :] if c < USED // P else dense_sb[:, c - USED // P, samples(k)]
                            got = mm(pU[:, P * m:P * (m + 1)], w1_sb[:, c, P * m:P * (m + 1)], rhs,
                                     start=c == 0, stop=c == NK - 1)
                    got.then_inc(h1_done, 1)
                if i == h2_step:
                    pe.wait_ge(h1_sb, count(k, 1, 1))
                    for m in range(H2 // P):
                        for c in range(H1 // P):
                            got = mm(pU[:, P * m:P * (m + 1)], w2_sb[:, c, P * m:P * (m + 1)], h1[:, c, :],
                                     start=c == 0, stop=c == H1 // P - 1)
                    got.then_inc(h2_done, 1)
                if i == o_step:
                    pe.wait_ge(h2_sb, count(k, 1, 1))
                    for c in range(H2 // P):
                        got = mm(pU[0:1, 0:P], col["w3"][:, c:c + 1], h2[:, c, :], start=c == 0, stop=c == H2 // P - 1)
                    got.then_inc(o_done, 1)

            pe.wait_ge(ld_dense, 16)
            pe.wait_ge(ld_wd, 16)
            for b in range(NBLK):
                for c in range(DENSE // P):
                    got = mm(pT[0][:, E * b:E * (b + 1)], dense_sb[:, c, P * b:P * (b + 1)], wd_sb[:, c, :],
                             start=c == 0, stop=c == DENSE // P - 1)
            got.then_inc(x_done, 1)
            pe.wait_ge(fills_ready, 1)
            pe.wait_ge(wexp_ready, 1)
            mm(pZ[0][:, 0:PJ], ones[0:NF, :], wsic[0:NF, 0, :], start=True, stop=True).then_inc(bias_done, 1)
            pe.wait_ge(x_norm, 1)
            pe.wait_ge(ld_const, 16)
            for b in range(NBLK):
                got = nc.tensor.transpose(pT[1][:, P * b:P * (b + 1)], xn[:, b, :], ident)
            got.then_inc(xT_done, 1)
            pe.wait_ge(xT_sb, 1)
            pe.wait_ge(bias_sb, 1)
            mm(pZ[0][64:65, :], ones[:, 0:1], xT[:], start=True, stop=True).then_inc(xsum_done, 1)
            pe.wait_ge(beye_ready, 1)
            pe.wait_ge(ld_wl, 16)
            for q in range(QG):
                got = mm(pU[32:64, :], beye[:, q, :], wl_sb[:, q, :], start=q == 0, stop=q == QG - 1)
            got.then_inc(wb_done, 1)
            pe.wait_ge(ld_wlx, 16)
            pe.wait_ge(wb_sb, 1)
            mm(pU[64:65, :], col["bp"][0:32, :], wlx_sb[:], start=True, stop=True)
            mm(pU[96:97, :], bp64[32:64, :], wbraw[32:64, :], start=True, stop=True).then_inc(wrow_done, 1)
            pe.wait_ge(wsc_ready, 1)
            pe.wait_ge(w_ready, 1)
            pe.wait_ge(xsum_sb, 1)
            pe.wait_ge(ld_w1, 32)
            pe.wait_ge(ld_w2, 16)
            run(pe, step)

        @block.scalar
        def _(act):
            def step(k, i):
                if i < NPAIR:
                    act.wait_ge(r_done, count(k, NPAIR, i + 1))
                    nc.scalar.copy(rowsT[:, i, :], pR[:, 0:P]).then_inc(r_sb, 1)
                for m in range(NBANK):
                    if i == bank_step[m]:
                        act.wait_ge(t1_sb, count(k, NBANK, m + 1))
                        nc.scalar.activation(t2[:, m], t1[:, m], ACT.Square).then_inc(t_sq, 1)
                j = i - 1
                if 0 <= j < NPAIR:
                    act.wait_ge(y_done, count(k, NPAIR, j + 1))
                    for c in range(2):
                        got = nc.scalar.activation(junk[:, c, :], pY[j % 2][:, E * c:E * (c + 1)], ACT.Square,
                                                   accum_out=yss[:, j, c:c + 1])
                    got.then_inc(y_sq, 1)
                    act.wait_ge(y_sq, count(k, NPAIR, j + 1))
                    nc.scalar.activation(ysd[:, j, :], yss[:, j, :], ACT.Sqrt, bias=eps[:], scale=1.0 / E).then_inc(y_std, 1)
                    act.wait_ge(y_rs, count(k, NPAIR, j + 1))
                    for c in range(2):
                        got = nc.scalar.activation(yn[:, j, c, :], pY[j % 2][:, E * c:E * (c + 1)], ACT.Copy,
                                                   scale=yrs[:, j, c:c + 1])
                    got.then_inc(y_sb, 1)
                for m in range(NBANK):
                    if i == bank_step[m]:
                        act.wait_ge(t_var, count(k, NBANK, m + 1))
                        nc.scalar.activation(tsd[:, m, :], tss[:, m, :], ACT.Sqrt, bias=eps[:], scale=1.0 / PJ).then_inc(t_std, 1)
                for half in range(2):
                    if i == z_step[2 * half] - 1:
                        if later(k):
                            act.wait_ge(z_done, count(k, NZ, 2 * half - 2))
                        g0 = 2 * ZQ * half
                        src = xT[:, samples(k)].rearrange("e (s g) -> e g s", s=4)[:, g0:g0 + 2 * ZQ, :]
                        dst = T[:, :, PJ].rearrange("e (g s) -> e g s", s=4)[:, g0:g0 + 2 * ZQ, :]
                        nc.scalar.copy(dst, src).then_inc(xcol_sb, 1)
                for h in range(NZ):
                    if i == z_step[h]:
                        act.wait_ge(z_done, count(k, NZ, h + 1))
                        if h == 0 and later(k):
                            act.wait_ge(zr_sb, count(k, 1, 0))
                            act.wait_ge(z9_sb, count(k, 1, 0))
                        nc.scalar.copy(zs[:, :, ZQ * h:ZQ * (h + 1)].rearrange("p q g -> p g q"),
                                       pZ[h % 2][:, 0:ZQ * NCOL].rearrange("p (g q) -> p g q", q=NCOL)).then_inc(zs_sb, 1)
                if i == zr_step:
                    act.wait_ge(zs_sb, count(k, NZ, NZ))
                    if later(k):
                        act.wait_ge(u_done, count(k, 1, 0))
                    for s in range(4):
                        for r in range(2):
                            nc.scalar.copy(z9[32 * r:32 * r + 32, QUADS * s:QUADS * (s + 1)],
                                           zs[32 * s:32 * s + 32, PJ + r, :])
                    nc.scalar.copy(z9[64:65, :], xsum[64:65, samples(k)]).then_inc(z9_sb, 1)
                if i == u_step + 1:
                    act.wait_ge(u_done, count(k, 1, 1))
                    nc.scalar.activation(ujunk[:], pU[:], ACT.Square, accum_out=uss[:]).then_inc(u_sq, 1)
                    act.wait_ge(u_sq, count(k, 1, 1))
                    nc.scalar.activation(usd[:], uss[:], ACT.Sqrt, bias=eps[:], scale=1.0 / UO).then_inc(u_std, 1)
                    act.wait_ge(u_rs, count(k, 1, 1))
                    nc.scalar.activation(un[:], pU[:, 0:USED], ACT.Copy, scale=urs[:]).then_inc(u_sb, 1)
                if i == zT_step:
                    act.wait_ge(zT_done, count(k, 1, 1))
                    for c in range(USED // P):
                        got = nc.scalar.activation(znT[:, c, :], pU[:, P * c:P * (c + 1)], ACT.Identity,
                                                   bias=col["bl"][:, c:c + 1], scale=col["gl"][:, c:c + 1])
                    got.then_inc(zT_sb, 1)
                if i == h1_step:
                    act.wait_ge(h1_done, count(k, 1, 1))
                    for m in range(H1 // P):
                        got = nc.scalar.activation(h1[:, m, :], pU[:, P * m:P * (m + 1)], ACT.Relu,
                                                   bias=col["b1"][:, m:m + 1])
                    got.then_inc(h1_sb, 1)
                if i == h2_step:
                    act.wait_ge(h2_done, count(k, 1, 1))
                    for m in range(H2 // P):
                        got = nc.scalar.activation(h2[:, m, :], pU[:, P * m:P * (m + 1)], ACT.Relu,
                                                   bias=col["b2"][:, m:m + 1])
                    got.then_inc(h2_sb, 1)
                if i == o_step:
                    act.wait_ge(o_done, count(k, 1, 1))
                    nc.scalar.copy(ysb[0:1, samples(k)], pU[0:1, 0:P]).then_inc(o_sb, 1)

            act.wait_ge(fills_ready, 1)
            act.wait_ge(x_var, 1)
            nc.scalar.activation(xsd[:], xmv[:, :, 1], ACT.Sqrt, bias=eps[:], scale=1.0).then_inc(x_std, 1)
            act.wait_ge(ld_cols, 16)
            act.wait_ge(xT_done, 1)
            nc.scalar.activation(xT[:], pT[1][:], ACT.Identity, bias=col["bd"], scale=col["gd"]).then_inc(xT_sb, 1)
            act.wait_ge(xsum_done, 1)
            nc.scalar.copy(xsum[64:65, :], pZ[0][64:65, :]).then_inc(xsum_sb, 1)
            run(act, step)

        @block.vector
        def _(dve):
            v = nc.vector

            def step(k, i):
                j = i - 1
                for m in range(NBANK):
                    if i == bank_step[m] + 1:
                        dve.wait_ge(t_std, count(k, NBANK, m + 1))
                        v.reciprocal(trs[:, m, :], tsd[:, m, :]).then_inc(t_rs, 1)
                        dve.wait_ge(t_rs, count(k, NBANK, m + 1))
                        if later(k):
                            dve.wait_ge(z_done, count(k, NZ, m // 2 + 1 - NZ if k[1] else 0))
                        v.tensor_tensor(T[:, SBANK * m:SBANK * (m + 1), 0:PJ], t1[:, m],
                                        trs[:, m, :].unsqueeze(2).to_broadcast([P, SBANK, PJ]), ALU.mult).then_inc(t_sb, 1)
                for m in range(NBANK):
                    if i == bank_step[m]:
                        dve.wait_ge(t_done, count(k, NBANK, m + 1))
                        v.scalar_tensor_tensor(out=t1[:, m], in0=pT[m % 2][:].rearrange("p (a b) -> p a b", b=PJ),
                                               scalar=col["gs"], in1=bias[:].unsqueeze(1).to_broadcast([P, SBANK, PJ]),
                                               op0=ALU.mult, op1=ALU.add).then_inc(t1_sb, 1)
                if 0 <= j < NPAIR:
                    dve.wait_ge(y_std, count(k, NPAIR, j + 1))
                    v.reciprocal(yrs[:, j, :], ysd[:, j, :]).then_inc(y_rs, 1)
                for m in range(NBANK):
                    if i == bank_step[m]:
                        dve.wait_ge(t_sq, count(k, NBANK, m + 1))
                        v.tensor_reduce(out=tss[:, m, :], in_=t2[:, m], op=ALU.add, axis=AX.X).then_inc(t_var, 1)
                if i == zr_step:
                    dve.wait_ge(zs_sb, count(k, NZ, NZ))
                    if later(k):
                        dve.wait_ge(u_done, count(k, 1, 0))
                    for s in range(4):
                        for r in range(4):
                            got = v.tensor_copy(zr[32 * r:32 * r + 32, :, QUADS * s:QUADS * (s + 1)],
                                                zs[32 * s:32 * s + 32, QG * r:QG * (r + 1), :])
                    got.then_inc(zr_sb, 1)
                if i == u_step + 1:
                    dve.wait_ge(u_std, count(k, 1, 1))
                    v.reciprocal(urs[:], usd[:]).then_inc(u_rs, 1)

            n = [0]

            def then(ins):
                n[0] += 1
                ins.then_inc(setup, 1)
                dve.wait_ge(setup, n[0])

            v.memset(eps[:], EPS)
            v.memset(ones[:], 1.0).then_inc(fills_ready, 1)
            v.memset(wsc[:], 0.0)
            dve.wait_ge(ld_index, 16)
            v.tensor_tensor(idx[:], idx_in[:, 0, :], idx_in[:, 1, :], ALU.add).then_inc(idx_ready, 1)
            dve.wait_ge(ld_ws, 16)
            then(v.tensor_reduce(out=wsm[:, 0:1], in_=ws_sb[:], op=ALU.add, axis=AX.X))
            then(v.tensor_scalar(wsm[:, 1:2], wsm[:, 0:1], 1.0 / E, None, ALU.mult))
            v.tensor_scalar(wsc[0:D, 0:E], ws_sb[0:D, :], wsm[0:D, 1:2], None, ALU.subtract)
            v.tensor_scalar(wsc[D:P, E:], ws_sb[D:P, :], wsm[D:P, 1:2], None, ALU.subtract).then_inc(wsc_ready, 1)
            dve.wait_ge(ld_wsi, 16)
            then(v.tensor_reduce(out=wsim[:, 0, :], in_=wsi_sb[:], op=ALU.add, axis=AX.X))
            then(v.tensor_scalar(wsim[:, 1, :], wsim[:, 0, :], 1.0 / PJ, None, ALU.mult))
            then(v.tensor_tensor(wsic[:], wsi_sb[:], wsim[:, 1, :].unsqueeze(2).to_broadcast([P, TW, PJ]), ALU.subtract))
            dve.wait_ge(ld_const, 16)
            for c in range(TW):
                got = v.tensor_tensor(wexp[:, c], wsic[:, c, :].unsqueeze(1).to_broadcast([P, SPAN, PJ]),
                                      mask[:, c, :].unsqueeze(2).to_broadcast([P, SPAN, PJ]), ALU.mult)
            got.then_inc(wexp_ready, 1)
            dve.wait_ge(ld_cols, 16)
            dve.wait_ge(bias_done, 1)
            v.tensor_scalar(bias[:], pZ[0][:, 0:PJ], col["bs"], None, ALU.mult).then_inc(bias_sb, 1)
            dve.wait_ge(x_done, 1)
            for b in range(NBLK):
                got = v.bn_stats(xstat[:, b, :], pT[0][:, E * b:E * (b + 1)])
            then(got)
            for b in range(NBLK):
                got = v.bn_aggr(xmv[:, b, :], xstat[:, b, :])
            got.then_inc(x_var, 1)
            dve.wait_ge(x_std, 1)
            then(v.reciprocal(xrs[:], xsd[:]))
            for b in range(NBLK):
                got = v.tensor_scalar(xn[:, b, :], pT[0][:, E * b:E * (b + 1)], xmv[:, b, 0:1], xrs[:, b:b + 1],
                                      ALU.subtract, ALU.mult)
            got.then_inc(x_norm, 1)
            v.memset(T[:, :, PJ + 1], 1.0)
            v.memset(z9[:], 0.0).then_inc(setup, 1)
            n[0] += 1
            dve.wait_ge(setup, n[0])
            v.memset(z9[96:97, :], 1.0)
            then(v.memset(w9[:], 0.0))
            for q in range(QG):
                got = v.tensor_scalar(beye[:, q, :], eye, col["bq"][:, q:q + 1], None, ALU.mult)
            got.then_inc(beye_ready, 1)
            then(v.tensor_scalar(gg[:], col["gq"], col["gp"], 0.5, ALU.mult, ALU.mult))
            v.tensor_scalar(bp64[:], col["bp"], float(E) / 2, None, ALU.mult)
            dve.wait_ge(ld_wl, 16)
            dve.wait_ge(ld_wlx, 16)
            then(v.tensor_reduce(out=wlm[:, 0, :], in_=wl_sb[:], op=ALU.add, axis=AX.X))
            then(v.tensor_scalar(wlm[:, 1, :], wlm[:, 0, :], 1.0 / UO, None, ALU.mult))
            for q in range(QG):
                v.tensor_scalar(wg[:, q, :], wl_sb[:, q, :], wlm[:, 1, q:q + 1], gg[:, q:q + 1], ALU.subtract, ALU.mult)
            v.tensor_scalar(w9[0:32, :], wlx_sb[:], col["gp"][0:32, :], None, ALU.mult)
            dve.wait_ge(wb_done, 1)
            v.tensor_copy(wbraw[32:64, :], pU[32:64, :]).then_inc(wb_sb, 1)
            v.tensor_scalar(w9[32:64, :], pU[32:64, :], col["gp"][32:64, :], None, ALU.mult)
            dve.wait_ge(wrow_done, 1)
            v.tensor_copy(w9[64:65, :], pU[64:65, :])
            then(v.tensor_copy(w9[96:97, :], pU[96:97, :]))
            then(v.tensor_reduce(out=w9m[:, 0:1], in_=w9[:], op=ALU.add, axis=AX.X))
            then(v.tensor_scalar(w9m[:, 1:2], w9m[:, 0:1], 1.0 / UO, None, ALU.mult))
            v.tensor_scalar(w9c[:], w9[:], w9m[:, 1:2], None, ALU.subtract).then_inc(w_ready, 1)
            run(dve, step)


def layout(inputs):
    a = {k: np.asarray(v) for k, v in inputs.items()}
    tables = np.concatenate([a[f"tbl_{f}"] for f in range(NF)], axis=0)
    first_row = np.concatenate([[0], np.cumsum(VOCAB)[:-1]]).astype(np.int32)
    r = np.arange(P * NC)
    t, n = r // NF, r % NF
    sample = (t % 4) * QUADS + t // 4
    ids = a["ids"].reshape(NBLK, P, NF)[:, sample, n].reshape(NBLK, NC, P).transpose(2, 0, 1).reshape(P, NBLK * NC)
    offs = np.broadcast_to(first_row[n].reshape(NC, P).T[:, None, :], (P, NBLK, NC)).reshape(P, NBLK * NC)
    index = np.stack([ids, offs], axis=1).astype(np.int32)
    mask = np.zeros((P, TW, SPAN), np.float32)
    for c in range(TW):
        for p in range(P):
            mask[p, c, (P * c + p) // NF - chunk_samples(c)[0]] = 1.0
    eye = np.tile(np.eye(PJ, dtype=np.float32), (4, 1))
    consts = np.concatenate([np.eye(P, dtype=np.float32), mask.reshape(P, -1), eye], axis=1)
    gsi, bsi = a["L0_rec_gsi"], a["L0_rec_bsi"]
    parts = {
        "bq": np.repeat(bsi.reshape(4, QG), PJ, axis=0), "gq": np.repeat(gsi.reshape(4, QG), PJ, axis=0),
        "bp": np.tile(bsi, 4)[:, None], "gp": np.tile(gsi, 4)[:, None],
        "gs": a["L0_rec_gs"][:, None], "bs": a["L0_rec_bs"][:, None],
        "gd": a["L0_rec_gd"][:, None], "bd": a["L0_rec_bd"][:, None],
        "gl": a["L0_rec_gl"][:USED].reshape(-1, P).T, "bl": a["L0_rec_bl"][:USED].reshape(-1, P).T,
        "b1": a["b_top1"].reshape(-1, P).T, "b2": a["b_top2"].reshape(-1, P).T,
        "w3": a["W_top3"].reshape(-1, P).T,
    }
    small = np.concatenate([parts[name] for name, _ in COLS], axis=1)
    ws_t = np.tile(a["L0_rec_Ws"].T, (2, 1))
    wsi_rows = a["L0_rec_Wsi"].T[n[:P * TW].reshape(TW, P).T]
    dense_t = a["r_dense_t"].T.reshape(DENSE // P, P, B).transpose(1, 0, 2)
    wd_t = a["L0_rec_Wd"].T.reshape(DENSE // P, P, E).transpose(1, 0, 2)
    pair = np.full((PJ, PJ), PJ * (PJ + 1) // 2)
    for p in range(PJ):
        for q in range(p):
            pair[p, q] = pair[q, p] = (p + 1) * p // 2 + q + 1
    wl_t = np.concatenate([a["L0_rec_Wl"].T, np.zeros((1, UO), np.float32)], axis=0)
    wl = wl_t[pair.reshape(PJ, 4, QG).transpose(1, 0, 2)].reshape(P, QG, UO)
    wlx = wl_t[[(p + 1) * p // 2 for p in range(PJ)]]
    return {"tables": tables, "index": index, "consts": consts, "small": small, "ws_t": ws_t, "wsi_rows": wsi_rows,
            "dense_t": dense_t, "wd_t": wd_t, "wl": wl, "wlx": wlx, "w1": a["W_top1"], "w2": a["W_top2"]}


def kernel(**inputs):
    import concourse.bacc as bacc
    from concourse.bass_utils import run_bass_kernel_spmd

    nc = bacc.Bacc("TRN2", target_bir_lowering=False, num_devices=1)
    arrays, args = {}, []
    for name, a in layout(inputs).items():
        a = np.ascontiguousarray(a)
        arrays[f"in_{name}"] = a
        args.append(nc.dram_tensor(f"in_{name}", a.shape, mybir.dt.from_np(a.dtype), kind="ExternalInput").ap())
    out = nc.dram_tensor("out_y", (B, 1), mybir.dt.float32, kind="ExternalOutput").ap()
    build(nc, *args, out.rearrange("b a -> a b"))
    return run_bass_kernel_spmd(nc, [arrays], core_ids=[0]).results[0]["out_y"]
```

```python
from contextlib import ExitStack

import numpy as np
import concourse.bass as bass
from concourse import mybir

VOCAB = [12500, 1000, 12500, 1000, 1000, 125000, 125000, 12500, 125000, 12500, 1000, 1250, 1000,
         12500, 1250, 1000, 12500, 1000, 1250, 1000, 1000, 1000, 1000, 12500, 12500, 1000]
B, NF, D, E, PJ = 512, len(VOCAB), 64, 128, 32
DENSE, UO, USED, H1, H2 = 256, 512, 384, 512, 256
P = 128
NBLK = B // P
NC = NF
NPAIR = NC // 2
SBANK = 512 // PJ
NBANK = P // SBANK
NCOL = PJ + 2
QUADS = P // 4
ZQ = 8
NZ = QUADS // ZQ
QG = PJ // 4
TW = 13
SPAN = 6
EPS = 1e-5

COLS = [("bq", QG), ("gq", QG), ("bp", 1), ("gp", 1), ("gs", 1), ("bs", 1), ("gd", 1), ("bd", 1),
        ("gl", USED // P), ("bl", USED // P), ("b1", H1 // P), ("b2", H2 // P), ("w3", H2 // P)]


def chunk_samples(c):
    return (P * c) // NF, (P * c + P - 1) // NF


def last_chunk(m):
    return (SBANK * NF * (m + 1) - 1) // P


def first_chunk(m):
    return (SBANK * NF * m) // P


def build(nc, tables, index, consts, small, ws_t, wsi_rows, dense_t, wd_t, wl, wlx, w1, w2, out):
    F32, I32 = mybir.dt.float32, mybir.dt.int32
    ALU, ACT, AX = mybir.AluOpType, mybir.ActivationFunctionType, mybir.AxisListType

    with ExitStack() as ctx:
        def sb(name, shape, dt=F32):
            return ctx.enter_context(nc.sbuf_tensor(name, shape, dt))

        def sem(name):
            return ctx.enter_context(nc.semaphore(name))

        def bank(name):
            return ctx.enter_context(nc.psum_tensor(name, [P, 512], F32))

        idx_in = sb("idx_in", [P, 2, NBLK * NC], I32)
        idx = sb("idx", [P, NBLK * NC], I32)
        const = sb("const", [P, P + TW * SPAN + PJ])
        cols = sb("cols", [P, sum(w for _, w in COLS)])
        ws_sb = sb("ws_sb", [P, E])
        wsi_sb = sb("wsi_sb", [P, TW, PJ])
        dense_sb = sb("dense_sb", [P, DENSE // P, B])
        wd_sb = sb("wd_sb", [P, DENSE // P, E])
        wl_sb = sb("wl_sb", [P, QG, UO])
        wlx_sb = sb("wlx_sb", [PJ, UO])
        w1_sb = sb("w1_sb", [P, (USED + DENSE) // P, H1])
        w2_sb = sb("w2_sb", [P, H1 // P, H2])
        ident = const[:, 0:P]
        mask = const[:, P:P + TW * SPAN].rearrange("p (c k) -> p c k", k=SPAN)
        eye = const[:, P + TW * SPAN:P + TW * SPAN + PJ]
        col = {}
        n = 0
        for name, width in COLS:
            col[name] = cols[:, n:n + width]
            n += width

        eps = sb("eps", [P, 1])
        ones = sb("ones", [P, P])
        wsm = sb("wsm", [P, 2])
        wsc = sb("wsc", [P, 2 * E])
        wsim = sb("wsim", [P, 2, TW])
        wsic = sb("wsic", [P, TW, PJ])
        wexp = sb("wexp", [P, TW, SPAN, PJ])
        bias = sb("bias", [P, PJ])
        gg = sb("gg", [P, QG])
        wg = sb("wg", [P, QG, UO])
        beye = sb("beye", [P, QG, PJ])
        bp64 = sb("bp64", [P, 1])
        w9 = sb("w9", [P, UO])
        w9c = sb("w9c", [P, UO])
        wlm = sb("wlm", [P, 2, QG])
        wljunk = sb("wljunk", [P, QG, UO])
        w9m = sb("w9m", [P, 2])
        wbraw = sb("wbraw", [P, UO])
        xstat = sb("xstat", [P, NBLK, 6])
        xmv = sb("xmv", [P, NBLK, 2])
        xsd = sb("xsd", [P, NBLK])
        xrs = sb("xrs", [P, NBLK])
        xn = sb("xn", [P, NBLK, E])
        xT = sb("xT", [P, B])
        xsum = sb("xsum", [P, B])
        rows = sb("rows", [P, NPAIR, 2 * D])
        rowsT = sb("rowsT", [P, NPAIR, P])
        junk = sb("junk", [P, 2, E])
        yss = sb("yss", [P, NPAIR, 2])
        ysd = sb("ysd", [P, NPAIR, 2])
        yrs = sb("yrs", [P, NPAIR, 2])
        yn = sb("yn", [P, NPAIR, 2, E])
        t1 = sb("t1", [P, NBANK, SBANK, PJ])
        t2 = sb("t2", [P, NBANK, SBANK, PJ])
        tss = sb("tss", [P, NBANK, SBANK])
        tsd = sb("tsd", [P, NBANK, SBANK])
        trs = sb("trs", [P, NBANK, SBANK])
        T = sb("T", [P, P, NCOL])
        zs = sb("zs", [P, NCOL, QUADS])
        zr = sb("zr", [P, QG, P])
        z9 = sb("z9", [P, P])
        ujunk = sb("ujunk", [P, UO])
        uss = sb("uss", [P, 1])
        usd = sb("usd", [P, 1])
        urs = sb("urs", [P, 1])
        un = sb("un", [P, USED])
        znT = sb("znT", [P, USED // P, P])
        h1 = sb("h1", [P, H1 // P, P])
        h2 = sb("h2", [P, H2 // P, P])
        ysb = sb("ysb", [1, B])

        pY = [bank("pY0"), bank("pY1"), bank("pY2")]
        pT = [bank("pT0"), bank("pT1")]
        pZ = bank("pZ")
        pU, pV = bank("pU"), bank("pV")

        ld_index, ld_const, ld_cols, ld_ws, ld_wsi = map(sem, ["ld_index", "ld_const", "ld_cols", "ld_ws", "ld_wsi"])
        ld_dense, ld_wd, ld_wl, ld_wlx, ld_w1, ld_w2 = map(
            sem, ["ld_dense", "ld_wd", "ld_wl", "ld_wlx", "ld_w1", "ld_w2"])
        idx_ready, fills_ready, wsc_ready, wexp_ready = map(sem, ["idx_ready", "fills_ready", "wsc_ready", "wexp_ready"])
        x_done, x_var, x_std, x_norm = map(sem, ["x_done", "x_var", "x_std", "x_norm"])
        xT_done, xT_sb, xsum_done, xsum_sb = map(sem, ["xT_done", "xT_sb", "xsum_done", "xsum_sb"])
        bias_done, bias_sb, beye_ready, wb_done, wb_sb, wrow_done, w_ready = map(
            sem, ["bias_done", "bias_sb", "beye_ready", "wb_done", "wb_sb", "wrow_done", "w_ready"])
        gathered = [sem(f"gathered{i}") for i in range(NPAIR)]
        r_done, r_sb, y_done, y_sq, y_std, y_rs, y_sb = map(
            sem, ["r_done", "r_sb", "y_done", "y_sq", "y_std", "y_rs", "y_sb"])
        t_done, t1_sb, t_sq, t_var, t_std, t_rs, t_sb, xcol_sb = map(
            sem, ["t_done", "t1_sb", "t_sq", "t_var", "t_std", "t_rs", "t_sb", "xcol_sb"])
        z_done, zs_sb, z9_sb, zr_sb = map(sem, ["z_done", "zs_sb", "z9_sb", "zr_sb"])
        u_done, u_sq, u_std, u_rs, u_sb = map(sem, ["u_done", "u_sq", "u_std", "u_rs", "u_sb"])
        zT_done, zT_sb, h1_done, h1_sb, h2_done, h2_sb, o_done, o_sb, out_done = map(
            sem, ["zT_done", "zT_sb", "h1_done", "h1_sb", "h2_done", "h2_sb", "o_done", "o_sb", "out_done"])
        wlm_sum = sem("wlm_sum")
        setup = sem("setup")

        block = ctx.enter_context(nc.Block())

        Y_LAG, NORM_LAG, YN_LAG, T_LAG = 2, 3, 4, 5
        bank_step = [last_chunk(m) // 2 + T_LAG for m in range(NBANK)]
        norm_step = [i + 1 for i in bank_step]
        scale_step = [i + 2 for i in bank_step]
        z_step = [bank_step[2 * h + 1] + 4 for h in range(NZ)]
        zr_steps = [{z_step[1] + 2: (0, 1), z_step[1] + 3: (2, 3)}, {z_step[3] + 1: (0, 1), z_step[3] + 2: (2, 3)}]
        u_first = z_step[3] + 4
        u_steps = {u_first: (0, 1), u_first + 1: (2, 3), u_first + 2: (4, 5), u_first + 3: (6,), u_first + 4: (7, QG)}
        norm_u = max(u_steps)
        zT_step = norm_u + 1
        h1_step = zT_step + 1
        h2_step = h1_step + H1 // P
        o_step = h2_step + 1
        STEPS = o_step + 1
        assert STEPS <= 3 * NPAIR
        NY = len(pY)
        assert (NPAIR - 1) % NY == 0

        def step_bank(i):
            return pV if i % NPAIR == NPAIR - 1 else pY[i % NPAIR % NY]

        def embedded(j):
            return step_bank(j + Y_LAG)[:, 0:2 * E]

        def transposed(i):
            return step_bank(i)[:, 2 * E:2 * E + P]

        def run(eng, step, prepare):
            def steps(i, blocks):
                for k, part in blocks:
                    if i + NPAIR * part < STEPS:
                        step(k, i + NPAIR * part)
            for i in range(NPAIR):
                steps(i, [((0, 0), 0)])
                if i in prepare:
                    prepare[i]()
            for i in range(NPAIR):
                steps(i, [((0, 0), 1), ((0, 1), 0)])
            with eng.Fori(0, NBLK - 2) as r:
                for i in range(NPAIR):
                    steps(i, [((r, 0), 2), ((r, 1), 1), ((r, 2), 0)])
            for i in range(NPAIR):
                steps(i, [((0, NBLK - 2), 2), ((0, NBLK - 1), 1)])
            for i in range(NPAIR):
                steps(i, [((0, NBLK - 1), 2)])

        ON_DVE = (3, 7, 11)

        def h1_part(m):
            return (pU, pV)[m // 2][:, P * (m % 2):P * (m % 2 + 1)]

        def count(k, per_block, n):
            return k[0] * per_block + (k[1] * per_block + n)

        def later(k, by=1):
            return not isinstance(k[0], int) or k[0] + k[1] >= by

        def last(k):
            return isinstance(k[0], int) and k[0] + k[1] == NBLK - 1

        def samples(k):
            return bass.ds(k[0] * P + k[1] * P, P)

        @block.sync
        def _(sp):
            for dst, src, done in [(idx_in[:], index, ld_index), (ws_sb[:], ws_t, ld_ws), (const[:], consts, ld_const),
                                   (wsi_sb[:], wsi_rows, ld_wsi), (cols[:], small, ld_cols),
                                   (dense_sb[:], dense_t, ld_dense), (wd_sb[:], wd_t, ld_wd), (wlx_sb[:], wlx, ld_wlx),
                                   (wl_sb[:], wl, ld_wl), (w1_sb[:, 0:USED // P, :],
                                                           w1[0:USED, :].rearrange("(c p) n -> p c n", p=P), ld_w1),
                                   (w1_sb[:, USED // P:, :],
                                    w1[UO:UO + DENSE, :].rearrange("(c p) n -> p c n", p=P), ld_w1),
                                   (w2_sb[:], w2.rearrange("(c p) n -> p c n", p=P), ld_w2)]:
                sp.dma_start(dst, src).then_inc(done, 16)
            sp.wait_ge(o_sb, NBLK)
            sp.dma_start(out, ysb[:]).then_inc(out_done, 16)
            sp.wait_ge(out_done, 16)

        @block.gpsimd
        def _(pool):
            pool.wait_ge(idx_ready, 1)
            for k in range(NBLK):
                for c in range(NC):
                    if k and c % 2 == 0:
                        pool.wait_ge(r_done, NPAIR * (k - 1) + c // 2 + 1)
                    pool.indirect_dma_start(
                        out=rows[:, c // 2, (c % 2) * D:(c % 2 + 1) * D], out_offset=None, in_=tables,
                        in_offset=bass.IndirectOffsetOnAxis(ap=idx[:, NC * k + c:NC * k + c + 1], axis=0),
                    ).then_inc(gathered[c // 2], 16)

        @block.tensor
        def _(pe):
            mm = nc.tensor.matmul

            def step(k, i):
                j = i - Y_LAG
                if 0 <= j < NPAIR:
                    before = [p for p in range(-NPAIR, j) if step_bank(p + Y_LAG) is step_bank(i)][-1]
                    if before >= 0 or later(k):
                        pe.wait_ge(y_sb, count(k, NPAIR, before + 1))
                    if i == NPAIR - 1 and later(k, 2):
                        pe.wait_ge(o_sb, count(k, 1, -1))
                    pe.wait_ge(r_sb, count(k, NPAIR, j + 1))
                    mm(embedded(j), rowsT[:, j, :], wsc[:], start=True, stop=True).then_inc(y_done, 1)
                if i < NPAIR:
                    pe.wait_ge(gathered[i], count(k, 32, 32))
                    nc.tensor.transpose(transposed(i), rows[:, i, :], ident).then_inc(r_done, 1)
                for h in range(NZ):
                    if i == z_step[h]:
                        pe.wait_ge(t_sb, count(k, NBANK, 2 * h + 2))
                        pe.wait_ge(xcol_sb, count(k, 2, h // 2 + 1))
                        if h or later(k):
                            pe.wait_ge(zs_sb, count(k, NZ, h))
                        for g in range(ZQ):
                            for s in range(4):
                                t = 4 * (ZQ * h + g) + s
                                got = mm(pZ[32 * s:32 * s + 32, NCOL * g:NCOL * (g + 1)], T[:, t, 0:PJ],
                                         T[:, t, :], start=True, stop=True)
                        got.then_inc(z_done, 1)
                if i in u_steps:
                    if 0 in u_steps[i]:
                        pe.wait_ge(zr_sb, count(k, 2, 2))
                    for q in u_steps[i]:
                        if q < QG:
                            mm(pU[:], zr[:, q, :], wg[:, q, :], start=q == 0, stop=False)
                        else:
                            pe.wait_ge(z9_sb, count(k, 2, 2))
                            mm(pU[:], z9[:], w9c[:], start=False, stop=True).then_inc(u_done, 1)
                if i == zT_step:
                    pe.wait_ge(u_sb, count(k, 1, 1))
                    if not last(k):
                        pe.wait_ge(y_sb, count(k, NPAIR, 2 * NPAIR - Y_LAG))
                    for c in range(USED // P):
                        got = nc.tensor.transpose(pV[:, P * c:P * (c + 1)], un[:, P * c:P * (c + 1)], ident)
                    got.then_inc(zT_done, 1)
                m = i - h1_step
                if 0 <= m < H1 // P:
                    if m == 0:
                        pe.wait_ge(zT_sb, count(k, 1, 1))
                    NK = (USED + DENSE) // P
                    for c in range(NK):
                        rhs = znT[:, c, :] if c < USED // P else dense_sb[:, c - USED // P, samples(k)]
                        got = mm(h1_part(m), w1_sb[:, c, P * m:P * (m + 1)], rhs, start=c == 0, stop=c == NK - 1)
                    if m % 2:
                        got.then_inc(h1_done, 1)
                if i == h2_step:
                    pe.wait_ge(h1_sb, count(k, 2, 2))
                    for m in range(H2 // P):
                        for c in range(H1 // P):
                            got = mm(pU[:, P * m:P * (m + 1)], w2_sb[:, c, P * m:P * (m + 1)], h1[:, c, :],
                                     start=c == 0, stop=c == H1 // P - 1)
                    got.then_inc(h2_done, 1)
                if i == o_step:
                    pe.wait_ge(h2_sb, count(k, 1, 1))
                    for c in range(H2 // P):
                        got = mm(pV[0:1, 0:P], col["w3"][:, c:c + 1], h2[:, c, :], start=c == 0, stop=c == H2 // P - 1)
                    got.then_inc(o_done, 1)
                j = i - T_LAG
                if 0 <= j < NPAIR:
                    pe.wait_ge(y_sb, count(k, NPAIR, j + 1))
                    for c in (2 * j, 2 * j + 1):
                        lo, hi = chunk_samples(c)
                        for m in range(lo // SBANK, hi // SBANK + 1):
                            a, z = max(lo, SBANK * m), min(hi, SBANK * (m + 1) - 1)
                            first = c == first_chunk(m)
                            if first and (m >= 2 or later(k)):
                                pe.wait_ge(t1_sb, count(k, NBANK, m - 1))
                            got = mm(pT[m % 2][:, PJ * (a - SBANK * m):PJ * (z + 1 - SBANK * m)], yn[:, j, c % 2, :],
                                     wexp[:, c % TW, a - lo:z + 1 - lo, :], start=first, stop=c == last_chunk(m),
                                     skip_group_check=True)
                            if c == last_chunk(m):
                                got.then_inc(t_done, 1)

            def dense():
                pe.wait_ge(ld_dense, 16)
                pe.wait_ge(ld_wd, 16)
                for b in range(NBLK):
                    for c in range(DENSE // P):
                        got = mm(pT[0][:, E * b:E * (b + 1)], dense_sb[:, c, P * b:P * (b + 1)], wd_sb[:, c, :],
                                 start=c == 0, stop=c == DENSE // P - 1)
                got.then_inc(x_done, 1)

            def dense_transposed():
                pe.wait_ge(x_norm, 1)
                for b in range(NBLK):
                    got = nc.tensor.transpose(pT[1][:, P * b:P * (b + 1)], xn[:, b, :], ident)
                got.then_inc(xT_done, 1)

            def dense_sums():
                pe.wait_ge(xT_sb, 1)
                pe.wait_ge(bias_sb, 1)
                mm(pZ[64:65, :], ones[:, 0:1], xT[:], start=True, stop=True).then_inc(xsum_done, 1)
                pe.wait_ge(wexp_ready, 1)

            def s_rows():
                pe.wait_ge(beye_ready, 1)
                pe.wait_ge(ld_wl, 16)
                pe.wait_ge(xsum_sb, 1)
                for q in range(QG):
                    got = mm(pZ[32:64, :], beye[:, q, :], wl_sb[:, q, :], start=q == 0, stop=q == QG - 1)
                got.then_inc(wb_done, 1)

            def single_rows():
                pe.wait_ge(ld_wlx, 16)
                pe.wait_ge(wb_sb, 1)
                mm(pZ[64:65, :], col["bp"][0:32, :], wlx_sb[:], start=True, stop=True)
                mm(pZ[96:97, :], bp64[32:64, :], wbraw[32:64, :], start=True, stop=True).then_inc(wrow_done, 1)

            def all_there():
                pe.wait_ge(w_ready, 1)
                pe.wait_ge(ld_w1, 32)
                pe.wait_ge(ld_w2, 16)

            pe.wait_ge(fills_ready, 1)
            pe.wait_ge(wexp_ready, 1)
            mm(pZ[:, 0:PJ], ones[0:NF, :], wsic[0:NF, 0, :], start=True, stop=True).then_inc(bias_done, 1)
            pe.wait_ge(ld_const, 16)
            pe.wait_ge(wsc_ready, 1)
            run(pe, step, {0: dense, 1: dense_transposed, 3: dense_sums, 5: s_rows, 7: single_rows, 10: all_there})

        @block.scalar
        def _(act):
            def step(k, i):
                j = i - YN_LAG
                if 0 <= j < NPAIR and j not in ON_DVE:
                    act.wait_ge(y_rs, count(k, NPAIR, j + 1))
                    for c in range(2):
                        got = nc.scalar.activation(yn[:, j, c, :], embedded(j)[:, E * c:E * (c + 1)], ACT.Copy,
                                                   scale=yrs[:, j, c:c + 1])
                    got.then_inc(y_sb, 1)
                for m in range(NBANK):
                    if i == scale_step[m]:
                        act.wait_ge(t_var, count(k, NBANK, m + 1))
                        nc.scalar.activation(tsd[:, m, :], tss[:, m, :], ACT.Sqrt, bias=eps[:], scale=1.0 / PJ).then_inc(t_std, 1)
                for m in range(NBANK):
                    if i == norm_step[m]:
                        act.wait_ge(t1_sb, count(k, NBANK, m + 1))
                        nc.scalar.activation(t2[:, m], t1[:, m], ACT.Square).then_inc(t_sq, 1)
                j = i - NORM_LAG
                if 0 <= j < NPAIR:
                    act.wait_ge(y_done, count(k, NPAIR, j + 1))
                    for c in range(2):
                        got = nc.scalar.activation(junk[:, c, :], embedded(j)[:, E * c:E * (c + 1)], ACT.Square,
                                                   accum_out=yss[:, j, c:c + 1])
                    got.then_inc(y_sq, 1)
                if i < NPAIR:
                    act.wait_ge(r_done, count(k, NPAIR, i + 1))
                    nc.scalar.copy(rowsT[:, i, :], transposed(i)).then_inc(r_sb, 1)
                if 0 <= j < NPAIR:
                    act.wait_ge(y_sq, count(k, NPAIR, j + 1))
                    nc.scalar.activation(ysd[:, j, :], yss[:, j, :], ACT.Sqrt, bias=eps[:], scale=1.0 / E).then_inc(y_std, 1)
                for half in range(2):
                    if i == z_step[2 * half] - 1:
                        g0 = 2 * ZQ * half
                        src = xT[:, samples(k)].rearrange("e (s g) -> e g s", s=4)[:, g0:g0 + 2 * ZQ, :]
                        dst = T[:, :, PJ].rearrange("e (g s) -> e g s", s=4)[:, g0:g0 + 2 * ZQ, :]
                        nc.scalar.copy(dst, src).then_inc(xcol_sb, 1)
                for h in range(NZ):
                    if i == z_step[h]:
                        act.wait_ge(z_done, count(k, NZ, h + 1))
                        if h == 0 and later(k):
                            act.wait_ge(zr_sb, count(k, 2, 0))
                            act.wait_ge(z9_sb, count(k, 2, 0))
                        nc.scalar.copy(zs[:, :, ZQ * h:ZQ * (h + 1)].rearrange("p q g -> p g q"),
                                       pZ[:, 0:ZQ * NCOL].rearrange("p (g q) -> p g q", q=NCOL)).then_inc(zs_sb, 1)
                for half in range(2):
                    if i in zr_steps[half]:
                        act.wait_ge(zs_sb, count(k, NZ, 2 * half + 2))
                        if 0 in zr_steps[half][i] and half == 0:
                            nc.scalar.copy(z9[64:65, :], xsum[64:65, samples(k)])
                        g0 = 2 * ZQ * half
                        for s in zr_steps[half][i]:
                            for r in range(2):
                                got = nc.scalar.copy(z9[32 * r:32 * r + 32, QUADS * s + g0:QUADS * s + g0 + 2 * ZQ],
                                                     zs[32 * s:32 * s + 32, PJ + r, g0:g0 + 2 * ZQ])
                        if s == 3:
                            got.then_inc(z9_sb, 1)
                if i == norm_u:
                    act.wait_ge(u_done, count(k, 1, 1))
                    nc.scalar.activation(ujunk[:], pU[:], ACT.Square, accum_out=uss[:]).then_inc(u_sq, 1)
                    act.wait_ge(u_sq, count(k, 1, 1))
                    nc.scalar.activation(usd[:], uss[:], ACT.Sqrt, bias=eps[:], scale=1.0 / UO).then_inc(u_std, 1)
                    act.wait_ge(u_rs, count(k, 1, 1))
                    nc.scalar.activation(un[:], pU[:, 0:USED], ACT.Copy, scale=urs[:]).then_inc(u_sb, 1)
                if i == zT_step:
                    act.wait_ge(zT_done, count(k, 1, 1))
                    for c in range(USED // P):
                        got = nc.scalar.activation(znT[:, c, :], pV[:, P * c:P * (c + 1)], ACT.Identity,
                                                   bias=col["bl"][:, c:c + 1], scale=col["gl"][:, c:c + 1])
                    got.then_inc(zT_sb, 1)
                m = i - h1_step
                if m in (1, 3):
                    act.wait_ge(h1_done, count(k, 2, m // 2 + 1))
                    for m in (m - 1, m):
                        got = nc.scalar.activation(h1[:, m, :], h1_part(m), ACT.Relu, bias=col["b1"][:, m:m + 1])
                    got.then_inc(h1_sb, 1)
                if i == h2_step:
                    act.wait_ge(h2_done, count(k, 1, 1))
                    for m in range(H2 // P):
                        got = nc.scalar.activation(h2[:, m, :], pU[:, P * m:P * (m + 1)], ACT.Relu,
                                                   bias=col["b2"][:, m:m + 1])
                    got.then_inc(h2_sb, 1)
                if i == o_step:
                    act.wait_ge(o_done, count(k, 1, 1))
                    nc.scalar.copy(ysb[0:1, samples(k)], pV[0:1, 0:P]).then_inc(o_sb, 1)

            def dense_deviation():
                act.wait_ge(x_var, 1)
                nc.scalar.activation(xsd[:], xmv[:, :, 1], ACT.Sqrt, bias=eps[:], scale=1.0).then_inc(x_std, 1)

            def dense_transposed():
                act.wait_ge(ld_cols, 16)
                act.wait_ge(xT_done, 1)
                nc.scalar.activation(xT[:], pT[1][:], ACT.Identity, bias=col["bd"], scale=col["gd"]).then_inc(xT_sb, 1)

            def sums():
                act.wait_ge(xsum_done, 1)
                nc.scalar.copy(xsum[64:65, :], pZ[64:65, :]).then_inc(xsum_sb, 1)
                act.wait_ge(ld_wl, 16)
                for q in range(QG):
                    got = nc.scalar.activation(wljunk[:, q, :], wl_sb[:, q, :], ACT.Copy, accum_out=wlm[:, 0, q:q + 1])
                got.then_inc(wlm_sum, 1)

            act.wait_ge(fills_ready, 1)
            run(act, step, {0: dense_deviation, 1: dense_transposed, 4: sums})

        @block.vector
        def _(dve):
            v = nc.vector

            def step(k, i):
                for m in range(NBANK):
                    if i == scale_step[m]:
                        dve.wait_ge(t_std, count(k, NBANK, m + 1))
                        v.reciprocal(trs[:, m, :], tsd[:, m, :]).then_inc(t_rs, 1)
                        dve.wait_ge(t_rs, count(k, NBANK, m + 1))
                        v.tensor_tensor(T[:, SBANK * m:SBANK * (m + 1), 0:PJ], t1[:, m],
                                        trs[:, m, :].unsqueeze(2).to_broadcast([P, SBANK, PJ]), ALU.mult).then_inc(t_sb, 1)
                j = i - NORM_LAG
                if 0 <= j < NPAIR:
                    dve.wait_ge(y_std, count(k, NPAIR, j + 1))
                    v.reciprocal(yrs[:, j, :], ysd[:, j, :]).then_inc(y_rs, 1)
                    if j in ON_DVE:
                        dve.wait_ge(y_rs, count(k, NPAIR, j + 1))
                        v.tensor_tensor(yn[:, j], embedded(j).rearrange("p (c e) -> p c e", e=E),
                                        yrs[:, j, :].unsqueeze(2).to_broadcast([P, 2, E]), ALU.mult).then_inc(y_sb, 1)
                for m in range(NBANK):
                    if i == norm_step[m]:
                        dve.wait_ge(t_sq, count(k, NBANK, m + 1))
                        v.tensor_reduce(out=tss[:, m, :], in_=t2[:, m], op=ALU.add, axis=AX.X).then_inc(t_var, 1)
                for half in range(2):
                    if i in zr_steps[half]:
                        dve.wait_ge(zs_sb, count(k, NZ, 2 * half + 2))
                        g0 = 2 * ZQ * half
                        for s in zr_steps[half][i]:
                            for r in range(4):
                                got = v.tensor_copy(zr[32 * r:32 * r + 32, :, QUADS * s + g0:QUADS * s + g0 + 2 * ZQ],
                                                    zs[32 * s:32 * s + 32, QG * r:QG * (r + 1), g0:g0 + 2 * ZQ])
                        if s == 3:
                            got.then_inc(zr_sb, 1)
                if i == norm_u:
                    dve.wait_ge(u_std, count(k, 1, 1))
                    v.reciprocal(urs[:], usd[:]).then_inc(u_rs, 1)
                for m in range(NBANK):
                    if i == bank_step[m]:
                        dve.wait_ge(t_done, count(k, NBANK, m + 1))
                        v.scalar_tensor_tensor(out=t1[:, m], in0=pT[m % 2][:].rearrange("p (a b) -> p a b", b=PJ),
                                               scalar=col["gs"], in1=bias[:].unsqueeze(1).to_broadcast([P, SBANK, PJ]),
                                               op0=ALU.mult, op1=ALU.add).then_inc(t1_sb, 1)

            n = [0]

            def then(ins):
                n[0] += 1
                ins.then_inc(setup, 1)
                dve.wait_ge(setup, n[0])

            def dense():
                dve.wait_ge(x_done, 1)
                for b in range(NBLK):
                    got = v.bn_stats(xstat[:, b, :], pT[0][:, E * b:E * (b + 1)])
                then(got)
                for b in range(NBLK):
                    got = v.bn_aggr(xmv[:, b, :], xstat[:, b, :])
                got.then_inc(x_var, 1)
                dve.wait_ge(x_std, 1)
                then(v.reciprocal(xrs[:], xsd[:]))
                for b in range(NBLK):
                    got = v.tensor_scalar(xn[:, b, :], pT[0][:, E * b:E * (b + 1)], xmv[:, b, 0:1], xrs[:, b:b + 1],
                                          ALU.subtract, ALU.mult)
                got.then_inc(x_norm, 1)
                dve.wait_ge(ld_cols, 16)
                dve.wait_ge(bias_done, 1)
                v.tensor_scalar(bias[:], pZ[:, 0:PJ], col["bs"], None, ALU.mult).then_inc(bias_sb, 1)
                for q in range(QG):
                    got = v.tensor_scalar(beye[:, q, :], eye, col["bq"][:, q:q + 1], None, ALU.mult)
                got.then_inc(beye_ready, 1)
                v.tensor_scalar(gg[:], col["gq"], col["gp"], 0.5, ALU.mult, ALU.mult)
                v.tensor_scalar(bp64[:], col["bp"], float(E) / 2, None, ALU.mult)
                v.memset(T[:, :, PJ + 1], 1.0)
                v.memset(w9[:], 0.0)
                then(v.memset(z9[:], 0.0))
                v.memset(z9[96:97, :], 1.0)

            def wl_rows():
                dve.wait_ge(wlm_sum, 1)
                then(v.tensor_scalar(wlm[:, 1, :], wlm[:, 0, :], 1.0 / UO, None, ALU.mult))
                for q in range(QG):
                    v.tensor_scalar(wg[:, q, :], wl_sb[:, q, :], wlm[:, 1, q:q + 1], gg[:, q:q + 1],
                                    ALU.subtract, ALU.mult)

            def s_rows():
                dve.wait_ge(wb_done, 1)
                v.tensor_copy(wbraw[32:64, :], pZ[32:64, :]).then_inc(wb_sb, 1)
                v.tensor_scalar(w9[32:64, :], pZ[32:64, :], col["gp"][32:64, :], None, ALU.mult)
                dve.wait_ge(ld_wlx, 16)
                v.tensor_scalar(w9[0:32, :], wlx_sb[:], col["gp"][0:32, :], None, ALU.mult)

            def single_rows():
                dve.wait_ge(wrow_done, 1)
                v.tensor_copy(w9[64:65, :], pZ[64:65, :])
                then(v.tensor_copy(w9[96:97, :], pZ[96:97, :]))
                then(v.tensor_reduce(out=w9m[:, 0:1], in_=w9[:], op=ALU.add, axis=AX.X))
                then(v.tensor_scalar(w9m[:, 1:2], w9m[:, 0:1], 1.0 / UO, None, ALU.mult))
                v.tensor_scalar(w9c[:], w9[:], w9m[:, 1:2], None, ALU.subtract).then_inc(w_ready, 1)

            v.memset(eps[:], EPS)
            v.memset(ones[:], 1.0).then_inc(fills_ready, 1)
            v.memset(wsc[:], 0.0)
            dve.wait_ge(ld_index, 16)
            v.tensor_tensor(idx[:], idx_in[:, 0, :], idx_in[:, 1, :], ALU.add).then_inc(idx_ready, 1)
            dve.wait_ge(ld_ws, 16)
            then(v.tensor_reduce(out=wsm[:, 0:1], in_=ws_sb[:], op=ALU.add, axis=AX.X))
            then(v.tensor_scalar(wsm[:, 1:2], wsm[:, 0:1], 1.0 / E, None, ALU.mult))
            v.tensor_scalar(wsc[0:D, 0:E], ws_sb[0:D, :], wsm[0:D, 1:2], None, ALU.subtract)
            v.tensor_scalar(wsc[D:P, E:], ws_sb[D:P, :], wsm[D:P, 1:2], None, ALU.subtract).then_inc(wsc_ready, 1)
            dve.wait_ge(ld_wsi, 16)
            then(v.tensor_reduce(out=wsim[:, 0, :], in_=wsi_sb[:], op=ALU.add, axis=AX.X))
            then(v.tensor_scalar(wsim[:, 1, :], wsim[:, 0, :], 1.0 / PJ, None, ALU.mult))
            then(v.tensor_tensor(wsic[:], wsi_sb[:], wsim[:, 1, :].unsqueeze(2).to_broadcast([P, TW, PJ]), ALU.subtract))
            dve.wait_ge(ld_const, 16)
            for c in range(TW):
                got = v.tensor_tensor(wexp[:, c], wsic[:, c, :].unsqueeze(1).to_broadcast([P, SPAN, PJ]),
                                      mask[:, c, :].unsqueeze(2).to_broadcast([P, SPAN, PJ]), ALU.mult)
            got.then_inc(wexp_ready, 1)
            run(dve, step, {0: dense, 6: wl_rows, 5: s_rows, 7: single_rows})


def layout(inputs):
    a = {k: np.asarray(v) for k, v in inputs.items()}
    tables = np.concatenate([a[f"tbl_{f}"] for f in range(NF)], axis=0)
    first_row = np.concatenate([[0], np.cumsum(VOCAB)[:-1]]).astype(np.int32)
    r = np.arange(P * NC)
    t, n = r // NF, r % NF
    sample = (t % 4) * QUADS + t // 4
    ids = a["ids"].reshape(NBLK, P, NF)[:, sample, n].reshape(NBLK, NC, P).transpose(2, 0, 1).reshape(P, NBLK * NC)
    offs = np.broadcast_to(first_row[n].reshape(NC, P).T[:, None, :], (P, NBLK, NC)).reshape(P, NBLK * NC)
    index = np.stack([ids, offs], axis=1).astype(np.int32)
    mask = np.zeros((P, TW, SPAN), np.float32)
    for c in range(TW):
        for p in range(P):
            mask[p, c, (P * c + p) // NF - chunk_samples(c)[0]] = 1.0
    eye = np.tile(np.eye(PJ, dtype=np.float32), (4, 1))
    consts = np.concatenate([np.eye(P, dtype=np.float32), mask.reshape(P, -1), eye], axis=1)
    gsi, bsi = a["L0_rec_gsi"], a["L0_rec_bsi"]
    parts = {
        "bq": np.repeat(bsi.reshape(4, QG), PJ, axis=0), "gq": np.repeat(gsi.reshape(4, QG), PJ, axis=0),
        "bp": np.tile(bsi, 4)[:, None], "gp": np.tile(gsi, 4)[:, None],
        "gs": a["L0_rec_gs"][:, None], "bs": a["L0_rec_bs"][:, None],
        "gd": a["L0_rec_gd"][:, None], "bd": a["L0_rec_bd"][:, None],
        "gl": a["L0_rec_gl"][:USED].reshape(-1, P).T, "bl": a["L0_rec_bl"][:USED].reshape(-1, P).T,
        "b1": a["b_top1"].reshape(-1, P).T, "b2": a["b_top2"].reshape(-1, P).T,
        "w3": a["W_top3"].reshape(-1, P).T,
    }
    small = np.concatenate([parts[name] for name, _ in COLS], axis=1)
    ws_t = np.tile(a["L0_rec_Ws"].T, (2, 1))
    wsi_rows = a["L0_rec_Wsi"].T[n[:P * TW].reshape(TW, P).T]
    dense_t = a["r_dense_t"].T.reshape(DENSE // P, P, B).transpose(1, 0, 2)
    wd_t = a["L0_rec_Wd"].T.reshape(DENSE // P, P, E).transpose(1, 0, 2)
    pair = np.full((PJ, PJ), PJ * (PJ + 1) // 2)
    for p in range(PJ):
        for q in range(p):
            pair[p, q] = pair[q, p] = (p + 1) * p // 2 + q + 1
    wl_t = np.concatenate([a["L0_rec_Wl"].T, np.zeros((1, UO), np.float32)], axis=0)
    wl = wl_t[pair.reshape(PJ, 4, QG).transpose(1, 0, 2)].reshape(P, QG, UO)
    wlx = wl_t[[(p + 1) * p // 2 for p in range(PJ)]]
    return {"tables": tables, "index": index, "consts": consts, "small": small, "ws_t": ws_t, "wsi_rows": wsi_rows,
            "dense_t": dense_t, "wd_t": wd_t, "wl": wl, "wlx": wlx, "w1": a["W_top1"], "w2": a["W_top2"]}


def kernel(**inputs):
    import concourse.bacc as bacc
    from concourse.bass_utils import run_bass_kernel_spmd

    nc = bacc.Bacc("TRN2", target_bir_lowering=False, num_devices=1)
    arrays, args = {}, []
    for name, a in layout(inputs).items():
        a = np.ascontiguousarray(a)
        arrays[f"in_{name}"] = a
        args.append(nc.dram_tensor(f"in_{name}", a.shape, mybir.dt.from_np(a.dtype), kind="ExternalInput").ap())
    out = nc.dram_tensor("out_y", (B, 1), mybir.dt.float32, kind="ExternalOutput").ap()
    build(nc, *args, out.rearrange("b a -> a b"))
    return run_bass_kernel_spmd(nc, [arrays], core_ids=[0]).results[0]["out_y"]
```

```python
import functools
from contextlib import ExitStack

import numpy as np
import concourse.bass as bass
from concourse import mybir

VOCAB = [12500, 1000, 12500, 1000, 1000, 125000, 125000, 12500, 125000, 12500, 1000, 1250, 1000,
         12500, 1250, 1000, 12500, 1000, 1250, 1000, 1000, 1000, 1000, 12500, 12500, 1000]
B, NF, D, E, PJ = 512, len(VOCAB), 64, 128, 32
DENSE, UO, USED, H1, H2 = 256, 512, 384, 512, 256
P = 128
NBLK = B // P
NC = NF
NPAIR = NC // 2
SBANK = 512 // PJ
NBANK = P // SBANK
NCOL = PJ + 2
QUADS = P // 4
ZQ = 8
NZ = QUADS // ZQ
QG = PJ // 4
TW = 13
SPAN = 6
EPS = 1e-5

COLS = [("bq", QG), ("gq", QG), ("bp", 1), ("gp", 1), ("gs", 1), ("bs", 1), ("gd", 1), ("bd", 1),
        ("gl", USED // P), ("bl", USED // P), ("b1", H1 // P), ("b2", H2 // P), ("w3", H2 // P)]


def chunk_samples(c):
    return (P * c) // NF, (P * c + P - 1) // NF


def last_chunk(m):
    return (SBANK * NF * (m + 1) - 1) // P


def first_chunk(m):
    return (SBANK * NF * m) // P


def build(nc, tables, index, consts, small, ws_t, wsi_rows, dense_t, wd_t, wl, wlx, w1, w2, out):
    F32, I32 = mybir.dt.float32, mybir.dt.int32
    ALU, ACT, AX = mybir.AluOpType, mybir.ActivationFunctionType, mybir.AxisListType

    with ExitStack() as ctx:
        def sb(name, shape, dt=F32):
            return ctx.enter_context(nc.sbuf_tensor(name, shape, dt))

        def sem(name):
            return ctx.enter_context(nc.semaphore(name))

        def bank(name):
            return ctx.enter_context(nc.psum_tensor(name, [P, 512], F32))

        idx_in = sb("idx_in", [P, 2, NBLK * NC], I32)
        idx = sb("idx", [P, NBLK * NC], I32)
        const = sb("const", [P, P + TW * SPAN + PJ])
        cols = sb("cols", [P, sum(w for _, w in COLS)])
        ws_sb = sb("ws_sb", [P, E])
        wsi_sb = sb("wsi_sb", [P, TW, PJ])
        dense_sb = sb("dense_sb", [P, DENSE // P, B])
        wd_sb = sb("wd_sb", [P, DENSE // P, E])
        wl_sb = sb("wl_sb", [P, QG, UO])
        wlx_sb = sb("wlx_sb", [PJ, UO])
        w1_sb = sb("w1_sb", [P, (USED + DENSE) // P, H1])
        w2_sb = sb("w2_sb", [P, H1 // P, H2])
        ident = const[:, 0:P]
        mask = const[:, P:P + TW * SPAN].rearrange("p (c k) -> p c k", k=SPAN)
        eye = const[:, P + TW * SPAN:P + TW * SPAN + PJ]
        col = {}
        n = 0
        for name, width in COLS:
            col[name] = cols[:, n:n + width]
            n += width

        eps = sb("eps", [P, 1])
        ones = sb("ones", [P, P])
        wsm = sb("wsm", [P, 2])
        wsc = sb("wsc", [P, 2 * E])
        wsim = sb("wsim", [P, 2, TW])
        wsic = sb("wsic", [P, TW, PJ])
        wexp = sb("wexp", [P, TW, SPAN, PJ])
        bias = sb("bias", [P, PJ])
        gg = sb("gg", [P, QG])
        wg = sb("wg", [P, QG, UO])
        beye = sb("beye", [P, QG, PJ])
        bp64 = sb("bp64", [P, 1])
        w9 = sb("w9", [P, UO])
        w9c = sb("w9c", [P, UO])
        wlm = sb("wlm", [P, 2, QG])
        wljunk = sb("wljunk", [P, QG, UO])
        w9m = sb("w9m", [P, 2])
        wbraw = sb("wbraw", [P, UO])
        xstat = sb("xstat", [P, NBLK, 6])
        xmv = sb("xmv", [P, NBLK, 2])
        xsd = sb("xsd", [P, NBLK])
        xrs = sb("xrs", [P, NBLK])
        xn = sb("xn", [P, NBLK, E])
        xT = sb("xT", [P, B])
        xsum = sb("xsum", [P, B])
        rows = sb("rows", [P, NPAIR, 2 * D])
        rowsT = sb("rowsT", [P, NPAIR, P])
        junk = sb("junk", [P, 2, E])
        yss = sb("yss", [P, NPAIR, 2])
        ysd = sb("ysd", [P, NPAIR, 2])
        yrs = sb("yrs", [P, NPAIR, 2])
        yn = sb("yn", [P, NPAIR, 2, E])
        t1 = sb("t1", [P, NBANK, SBANK, PJ])
        t2 = sb("t2", [P, NBANK, SBANK, PJ])
        tss = sb("tss", [P, NBANK, SBANK])
        tsd = sb("tsd", [P, NBANK, SBANK])
        trs = sb("trs", [P, NBANK, SBANK])
        T = sb("T", [P, P, NCOL])
        zs = sb("zs", [P, NCOL, QUADS])
        zr = sb("zr", [P, QG, P])
        z9 = sb("z9", [P, P])
        ujunk = sb("ujunk", [P, UO])
        uss = sb("uss", [P, 1])
        usd = sb("usd", [P, 1])
        urs = sb("urs", [P, 1])
        un = sb("un", [P, USED])
        znT = sb("znT", [P, USED // P, P])
        h1 = sb("h1", [P, H1 // P, P])
        h2 = sb("h2", [P, H2 // P, P])
        ysb = sb("ysb", [1, B])

        pY = [bank("pY0"), bank("pY1"), bank("pY2")]
        pT = [bank("pT0"), bank("pT1")]
        pZ = bank("pZ")
        pU, pV = bank("pU"), bank("pV")

        ld_index, ld_const, ld_cols, ld_ws, ld_wsi = map(sem, ["ld_index", "ld_const", "ld_cols", "ld_ws", "ld_wsi"])
        ld_dense, ld_wd, ld_wl, ld_wlx, ld_w1, ld_w2 = map(
            sem, ["ld_dense", "ld_wd", "ld_wl", "ld_wlx", "ld_w1", "ld_w2"])
        idx_ready, fills_ready, wsc_ready, wsic_ready, wexp_ready = map(sem, ["idx_ready", "fills_ready", "wsc_ready", "wsic_ready", "wexp_ready"])
        x_done, x_var, x_std, x_norm = map(sem, ["x_done", "x_var", "x_std", "x_norm"])
        xT_done, xT_sb, xsum_done, xsum_sb = map(sem, ["xT_done", "xT_sb", "xsum_done", "xsum_sb"])
        bias_done, bias_sb, beye_ready, wb_done, wb_sb, wrow_done, w9_ready, w_ready = map(
            sem, ["bias_done", "bias_sb", "beye_ready", "wb_done", "wb_sb", "wrow_done", "w9_ready", "w_ready"])
        gathered = [sem(f"gathered{i}") for i in range(NPAIR)]
        r_done, r_sb, y_done, y_sq, y_std, y_rs, y_sb = map(
            sem, ["r_done", "r_sb", "y_done", "y_sq", "y_std", "y_rs", "y_sb"])
        t_done, t1_sb, t_sq, t_var, t_std, t_rs, t_sb, xcol_sb, xrow_sb = map(
            sem, ["t_done", "t1_sb", "t_sq", "t_var", "t_std", "t_rs", "t_sb", "xcol_sb", "xrow_sb"])
        z_done, zs_sb, z9_sb, zr_sb = map(sem, ["z_done", "zs_sb", "z9_sb", "zr_sb"])
        u_done, u_sq, u_std, u_rs, u_sb = map(sem, ["u_done", "u_sq", "u_std", "u_rs", "u_sb"])
        zT_done, zT_sb, h1_done, h1_sb, h2_done, h2_sb, o_done, o_sb, out_done = map(
            sem, ["zT_done", "zT_sb", "h1_done", "h1_sb", "h2_done", "h2_sb", "o_done", "o_sb", "out_done"])
        wlm_sum = sem("wlm_sum")
        setup = sem("setup")

        block = ctx.enter_context(nc.Block())

        Y_LAG, NORM_LAG, YN_LAG, T_LAG = 2, 3, 4, 5
        bank_step = [last_chunk(m) // 2 + T_LAG for m in range(NBANK)]
        norm_step = [i + 1 for i in bank_step]
        scale_step = [i + 2 for i in bank_step]
        z_step = [bank_step[2 * h + 1] + slack for h, slack in enumerate((5, 5, 4, 4))]
        zr_steps = [{z_step[1] + 3: (0, 1), z_step[1] + 4: (2, 3)}, {z_step[3] + 1: (0, 1, 2), z_step[3] + 2: (3,)}]
        u_first = z_step[3] + 4
        u_steps = {u_first: (0, 1), u_first + 1: (2, 3), u_first + 2: (4, 5), u_first + 3: (6,), u_first + 4: (7, QG)}
        norm_u = max(u_steps)
        zT_step = norm_u + 1
        h1_step = zT_step + 1
        h2_step = h1_step + H1 // P
        o_step = h2_step + 1
        STEPS = o_step + 1
        assert STEPS <= 3 * NPAIR
        NY = len(pY)
        assert (NPAIR - 1) % NY == 0

        S_ROWS, WL_STEP = 9, 12

        def step_bank(i):
            return pV if i % NPAIR == NPAIR - 1 else pY[i % NPAIR % NY]

        def embedded(j):
            return step_bank(j + Y_LAG)[:, 0:2 * E]

        def transposed(i):
            return step_bank(i)[:, 2 * E:2 * E + P]

        def run(eng, step, prepare):
            def steps(i, blocks):
                for k, part in blocks:
                    if i + NPAIR * part < STEPS:
                        step(k, i + NPAIR * part)
            for i in range(NPAIR):
                steps(i, [((0, 0), 0)])
                if i in prepare:
                    prepare[i]()
            for i in range(NPAIR):
                steps(i, [((0, 0), 1), ((0, 1), 0)])
                if i + NPAIR in prepare:
                    prepare[i + NPAIR]()
            with eng.Fori(0, NBLK - 2) as r:
                for i in range(NPAIR):
                    steps(i, [((r, 0), 2), ((r, 1), 1), ((r, 2), 0)])
            for i in range(NPAIR):
                steps(i, [((0, NBLK - 2), 2), ((0, NBLK - 1), 1)])
            for i in range(NPAIR):
                steps(i, [((0, NBLK - 1), 2)])

        def h1_part(m):
            return (pU, pV)[m // 2][:, P * (m % 2):P * (m % 2 + 1)]

        def count(k, per_block, n):
            return k[0] * per_block + (k[1] * per_block + n)

        def later(k, by=1):
            return not isinstance(k[0], int) or k[0] + k[1] >= by

        def last(k):
            return isinstance(k[0], int) and k[0] + k[1] == NBLK - 1

        def samples(k):
            return bass.ds(k[0] * P + k[1] * P, P)

        @block.sync
        def _(sp):
            for dst, src, done in [(idx_in[:], index, ld_index), (const[:], consts, ld_const), (ws_sb[:], ws_t, ld_ws),
                                   (wsi_sb[:], wsi_rows, ld_wsi), (cols[:], small, ld_cols)]:
                sp.dma_start(dst, src).then_inc(done, 16)
            sp.wait_ge(ld_const, 16)
            for dst, src, done in [(dense_sb[:], dense_t, ld_dense), (wd_sb[:], wd_t, ld_wd), (wlx_sb[:], wlx, ld_wlx)]:
                sp.dma_start(dst, src).then_inc(done, 16)
            for q in range(0, QG, 2):
                sp.wait_ge(r_done, 2 + q // 2)
                sp.dma_start(wl_sb[:, q:q + 2, :], wl[:, q:q + 2, :]).then_inc(ld_wl, 16)
            for c in range((USED + DENSE) // P):
                sp.wait_ge(r_done, 6 + c)
                first = P * c if P * c < USED else P * c + UO - USED
                sp.dma_start(w1_sb[:, c, :], w1[first:first + P, :]).then_inc(ld_w1, 16)
            sp.dma_start(w2_sb[:], w2.rearrange("(c p) n -> p c n", p=P)).then_inc(ld_w2, 16)
            with sp.Fori(0, NBLK) as k:
                sp.wait_ge(zs_sb, k * NZ + NZ)
                for s in range(4):
                    for r in range(2):
                        sp.dma_start(z9[32 * r:32 * r + 32, QUADS * s:QUADS * (s + 1)],
                                     zs[32 * s:32 * s + 32, PJ + r, :]).then_inc(z9_sb, 16)
            sp.wait_ge(o_sb, NBLK)
            sp.dma_start(out, ysb[:]).then_inc(out_done, 16)
            sp.wait_ge(out_done, 16)

        @block.gpsimd
        def _(pool):
            pool.wait_ge(idx_ready, 1)
            for k in range(NBLK):
                for c in range(NC):
                    if k and c % 2 == 0:
                        pool.wait_ge(r_done, NPAIR * (k - 1) + c // 2 + 1)
                    pool.indirect_dma_start(
                        out=rows[:, c // 2, (c % 2) * D:(c % 2 + 1) * D], out_offset=None, in_=tables,
                        in_offset=bass.IndirectOffsetOnAxis(ap=idx[:, NC * k + c:NC * k + c + 1], axis=0),
                    ).then_inc(gathered[c // 2], 16)

        @block.tensor
        def _(pe):
            mm = nc.tensor.matmul

            def step(k, i):
                j = i - Y_LAG
                if 0 <= j < NPAIR:
                    before = [p for p in range(-NPAIR, j) if step_bank(p + Y_LAG) is step_bank(i)][-1]
                    if before >= 0 or later(k):
                        pe.wait_ge(y_sb, count(k, NPAIR, before + 1))
                    if i == NPAIR - 1 and later(k, 2):
                        pe.wait_ge(o_sb, count(k, 1, -1))
                    pe.wait_ge(r_sb, count(k, NPAIR, j + 1))
                    mm(embedded(j), rowsT[:, j, :], wsc[:], start=True, stop=True).then_inc(y_done, 1)
                if i < NPAIR:
                    pe.wait_ge(gathered[i], count(k, 32, 32))
                    nc.tensor.transpose(transposed(i), rows[:, i, :], ident).then_inc(r_done, 1)
                for h in range(NZ):
                    if i == z_step[h]:
                        pe.wait_ge(t_sb, count(k, NBANK, 2 * h + 2))
                        pe.wait_ge(xcol_sb, count(k, 2, h // 2 + 1))
                        if h or later(k):
                            pe.wait_ge(zs_sb, count(k, NZ, h))
                        for g in range(ZQ):
                            for s in range(4):
                                t = 4 * (ZQ * h + g) + s
                                got = mm(pZ[32 * s:32 * s + 32, NCOL * g:NCOL * (g + 1)], T[:, t, 0:PJ],
                                         T[:, t, :], start=True, stop=True)
                        got.then_inc(z_done, 1)
                if i in u_steps:
                    if 0 in u_steps[i]:
                        pe.wait_ge(zr_sb, count(k, 2, 2))
                    for q in u_steps[i]:
                        if q < QG:
                            mm(pU[:], zr[:, q, :], wg[:, q, :], start=q == 0, stop=False)
                        else:
                            pe.wait_ge(z9_sb, count(k, 128, 128))
                            pe.wait_ge(xrow_sb, count(k, 1, 1))
                            mm(pU[:], z9[:], w9c[:], start=False, stop=True).then_inc(u_done, 1)
                if i == zT_step:
                    pe.wait_ge(u_sb, count(k, 1, 1))
                    if not last(k):
                        pe.wait_ge(y_sb, count(k, NPAIR, 2 * NPAIR - Y_LAG))
                    for c in range(USED // P):
                        got = nc.tensor.transpose(pV[:, P * c:P * (c + 1)], un[:, P * c:P * (c + 1)], ident)
                    got.then_inc(zT_done, 1)
                m = i - h1_step
                if 0 <= m < H1 // P:
                    if m == 0:
                        pe.wait_ge(zT_sb, count(k, 1, 1))
                    NK = (USED + DENSE) // P
                    for c in range(NK):
                        rhs = znT[:, c, :] if c < USED // P else dense_sb[:, c - USED // P, samples(k)]
                        got = mm(h1_part(m), w1_sb[:, c, P * m:P * (m + 1)], rhs, start=c == 0, stop=c == NK - 1)
                    if m % 2:
                        got.then_inc(h1_done, 1)
                if i == h2_step:
                    pe.wait_ge(h1_sb, count(k, 2, 2))
                    for m in range(H2 // P):
                        for c in range(H1 // P):
                            got = mm(pU[:, P * m:P * (m + 1)], w2_sb[:, c, P * m:P * (m + 1)], h1[:, c, :],
                                     start=c == 0, stop=c == H1 // P - 1)
                    got.then_inc(h2_done, 1)
                if i == o_step:
                    pe.wait_ge(h2_sb, count(k, 1, 1))
                    for c in range(H2 // P):
                        got = mm(pV[0:1, 0:P], col["w3"][:, c:c + 1], h2[:, c, :], start=c == 0, stop=c == H2 // P - 1)
                    got.then_inc(o_done, 1)
                j = i - T_LAG
                if 0 <= j < NPAIR:
                    pe.wait_ge(y_sb, count(k, NPAIR, j + 1))
                    for c in (2 * j, 2 * j + 1):
                        lo, hi = chunk_samples(c)
                        for m in range(lo // SBANK, hi // SBANK + 1):
                            a, z = max(lo, SBANK * m), min(hi, SBANK * (m + 1) - 1)
                            first = c == first_chunk(m)
                            if first and (m >= 2 or later(k)):
                                pe.wait_ge(t1_sb, count(k, NBANK, m - 1))
                            got = mm(pT[m % 2][:, PJ * (a - SBANK * m):PJ * (z + 1 - SBANK * m)], yn[:, j, c % 2, :],
                                     wexp[:, c % TW, a - lo:z + 1 - lo, :], start=first, stop=c == last_chunk(m),
                                     skip_group_check=True)
                            if c == last_chunk(m):
                                got.then_inc(t_done, 1)

            def row_bias():
                pe.wait_ge(wsic_ready, 1)
                mm(pZ[:, 0:PJ], ones[0:NF, :], wsic[0:NF, 0, :], start=True, stop=True).then_inc(bias_done, 1)

            def dense(b):
                pe.wait_ge(ld_dense, 16)
                pe.wait_ge(ld_wd, 16)
                for c in range(DENSE // P):
                    got = mm(pU[:, E * b:E * (b + 1)], dense_sb[:, c, P * b:P * (b + 1)], wd_sb[:, c, :],
                             start=c == 0, stop=c == DENSE // P - 1)
                if b == NBLK - 1:
                    got.then_inc(x_done, 1)
                    pe.wait_ge(wexp_ready, 1)

            def dense_transposed():
                pe.wait_ge(x_norm, 1)
                for b in range(NBLK):
                    got = nc.tensor.transpose(pV[:, P * b:P * (b + 1)], xn[:, b, :], ident)
                got.then_inc(xT_done, 1)

            def dense_sums():
                pe.wait_ge(xT_sb, 1)
                pe.wait_ge(bias_sb, 1)
                mm(pZ[64:65, :], ones[:, 0:1], xT[:], start=True, stop=True).then_inc(xsum_done, 1)

            def s_rows():
                pe.wait_ge(beye_ready, 1)
                pe.wait_ge(ld_wl, 16 * QG // 2)
                for q in range(QG):
                    got = mm(pU[32:64, :], beye[:, q, :], wl_sb[:, q, :], start=q == 0, stop=q == QG - 1)
                got.then_inc(wb_done, 1)

            def single_rows():
                pe.wait_ge(ld_wlx, 16)
                pe.wait_ge(wb_sb, 1)
                mm(pU[64:65, :], col["bp"][0:32, :], wlx_sb[:], start=True, stop=True)
                mm(pU[96:97, :], bp64[32:64, :], wbraw[32:64, :], start=True, stop=True).then_inc(wrow_done, 1)

            def late_weights():
                pe.wait_ge(w9_ready, 1)
                pe.wait_ge(w_ready, QG)
                pe.wait_ge(ld_w1, 16 * (USED + DENSE) // P)
                pe.wait_ge(ld_w2, 16)

            pe.wait_ge(ld_const, 16)
            pe.wait_ge(wsc_ready, 1)
            pe.wait_ge(fills_ready, 1)
            run(pe, step, {0: row_bias, **{1 + b: functools.partial(dense, b) for b in range(NBLK)},
                           NBLK + 3: dense_transposed, NBLK + 4: dense_sums, S_ROWS: s_rows, S_ROWS + 3: single_rows,
                           u_first - 1: late_weights})

        @block.scalar
        def _(act):
            def step(k, i):
                j = i - YN_LAG
                if 0 <= j < NPAIR:
                    act.wait_ge(y_rs, count(k, NPAIR, j + 1))
                    for c in range(2):
                        got = nc.scalar.activation(yn[:, j, c, :], embedded(j)[:, E * c:E * (c + 1)], ACT.Copy,
                                                   scale=yrs[:, j, c:c + 1])
                    got.then_inc(y_sb, 1)
                for m in range(NBANK):
                    if i == scale_step[m]:
                        act.wait_ge(t_var, count(k, NBANK, m + 1))
                        nc.scalar.activation(tsd[:, m, :], tss[:, m, :], ACT.Sqrt, bias=eps[:], scale=1.0 / PJ).then_inc(t_std, 1)
                for m in range(NBANK):
                    if i == norm_step[m]:
                        act.wait_ge(t1_sb, count(k, NBANK, m + 1))
                        nc.scalar.activation(t2[:, m], t1[:, m], ACT.Square).then_inc(t_sq, 1)
                j = i - NORM_LAG
                if 0 <= j < NPAIR:
                    act.wait_ge(y_done, count(k, NPAIR, j + 1))
                    for c in range(2):
                        got = nc.scalar.activation(junk[:, c, :], embedded(j)[:, E * c:E * (c + 1)], ACT.Square,
                                                   accum_out=yss[:, j, c:c + 1])
                    got.then_inc(y_sq, 1)
                if 0 <= j < NPAIR:
                    act.wait_ge(y_sq, count(k, NPAIR, j + 1))
                    nc.scalar.activation(ysd[:, j, :], yss[:, j, :], ACT.Sqrt, bias=eps[:], scale=1.0 / E).then_inc(y_std, 1)
                if i < NPAIR:
                    act.wait_ge(r_done, count(k, NPAIR, i + 1))
                    nc.scalar.copy(rowsT[:, i, :], transposed(i)).then_inc(r_sb, 1)
                for half in range(2):
                    if i == z_step[2 * half] - 1:
                        g0 = 2 * ZQ * half
                        src = xT[:, samples(k)].rearrange("e (s g) -> e g s", s=4)[:, g0:g0 + 2 * ZQ, :]
                        dst = T[:, :, PJ].rearrange("e (g s) -> e g s", s=4)[:, g0:g0 + 2 * ZQ, :]
                        nc.scalar.copy(dst, src).then_inc(xcol_sb, 1)
                for h in range(NZ):
                    if i == z_step[h]:
                        act.wait_ge(z_done, count(k, NZ, h + 1))
                        if h == 0 and later(k):
                            act.wait_ge(zr_sb, count(k, 2, 0))
                            act.wait_ge(z9_sb, count(k, 128, 0))
                        nc.scalar.copy(zs[:, :, ZQ * h:ZQ * (h + 1)].rearrange("p q g -> p g q"),
                                       pZ[:, 0:ZQ * NCOL].rearrange("p (g q) -> p g q", q=NCOL)).then_inc(zs_sb, 1)
                if i == z_step[-1]:
                    nc.scalar.copy(z9[64:65, :], xsum[64:65, samples(k)]).then_inc(xrow_sb, 1)
                if i == norm_u:
                    act.wait_ge(u_done, count(k, 1, 1))
                    nc.scalar.activation(ujunk[:], pU[:], ACT.Square, accum_out=uss[:]).then_inc(u_sq, 1)
                    act.wait_ge(u_sq, count(k, 1, 1))
                    nc.scalar.activation(usd[:], uss[:], ACT.Sqrt, bias=eps[:], scale=1.0 / UO).then_inc(u_std, 1)
                    act.wait_ge(u_rs, count(k, 1, 1))
                    nc.scalar.activation(un[:], pU[:, 0:USED], ACT.Copy, scale=urs[:]).then_inc(u_sb, 1)
                if i == zT_step:
                    act.wait_ge(zT_done, count(k, 1, 1))
                    for c in range(USED // P):
                        got = nc.scalar.activation(znT[:, c, :], pV[:, P * c:P * (c + 1)], ACT.Identity,
                                                   bias=col["bl"][:, c:c + 1], scale=col["gl"][:, c:c + 1])
                    got.then_inc(zT_sb, 1)
                m = i - h1_step
                if m in (1, 3):
                    act.wait_ge(h1_done, count(k, 2, m // 2 + 1))
                    for m in (m - 1, m):
                        got = nc.scalar.activation(h1[:, m, :], h1_part(m), ACT.Relu, bias=col["b1"][:, m:m + 1])
                    got.then_inc(h1_sb, 1)
                if i == h2_step:
                    act.wait_ge(h2_done, count(k, 1, 1))
                    for m in range(H2 // P):
                        got = nc.scalar.activation(h2[:, m, :], pU[:, P * m:P * (m + 1)], ACT.Relu,
                                                   bias=col["b2"][:, m:m + 1])
                    got.then_inc(h2_sb, 1)
                if i == o_step:
                    act.wait_ge(o_done, count(k, 1, 1))
                    nc.scalar.copy(ysb[0:1, samples(k)], pV[0:1, 0:P]).then_inc(o_sb, 1)

            def dense_deviation():
                act.wait_ge(x_var, 1)
                nc.scalar.activation(xsd[:], xmv[:, :, 1], ACT.Sqrt, bias=eps[:], scale=1.0).then_inc(x_std, 1)

            def dense_transposed():
                act.wait_ge(ld_cols, 16)
                act.wait_ge(xT_done, 1)
                nc.scalar.activation(xT[:], pV[:], ACT.Identity, bias=col["bd"], scale=col["gd"]).then_inc(xT_sb, 1)

            def dense_sums():
                act.wait_ge(xsum_done, 1)
                nc.scalar.copy(xsum[64:65, :], pZ[64:65, :]).then_inc(xsum_sb, 1)

            def wl_sum(q):
                act.wait_ge(ld_wl, 16 * (q // 2 + 1))
                nc.scalar.activation(wljunk[:, q, :], wl_sb[:, q, :], ACT.Copy,
                                     accum_out=wlm[:, 0, q:q + 1]).then_inc(wlm_sum, 1)

            act.wait_ge(fills_ready, 1)
            run(act, step, {NBLK + 1: dense_deviation, NBLK + 3: dense_transposed, NBLK + 4: dense_sums,
                            **{WL_STEP + q: functools.partial(wl_sum, q) for q in range(QG)}})

        @block.vector
        def _(dve):
            v = nc.vector

            def step(k, i):
                for m in range(NBANK):
                    if i == scale_step[m]:
                        dve.wait_ge(t_std, count(k, NBANK, m + 1))
                        v.reciprocal(trs[:, m, :], tsd[:, m, :]).then_inc(t_rs, 1)
                        dve.wait_ge(t_rs, count(k, NBANK, m + 1))
                        v.tensor_tensor(T[:, SBANK * m:SBANK * (m + 1), 0:PJ], t1[:, m],
                                        trs[:, m, :].unsqueeze(2).to_broadcast([P, SBANK, PJ]), ALU.mult).then_inc(t_sb, 1)
                j = i - NORM_LAG
                if 0 <= j < NPAIR:
                    dve.wait_ge(y_std, count(k, NPAIR, j + 1))
                    v.reciprocal(yrs[:, j, :], ysd[:, j, :]).then_inc(y_rs, 1)
                for m in range(NBANK):
                    if i == norm_step[m]:
                        dve.wait_ge(t_sq, count(k, NBANK, m + 1))
                        v.tensor_reduce(out=tss[:, m, :], in_=t2[:, m], op=ALU.add, axis=AX.X).then_inc(t_var, 1)
                for half in range(2):
                    if i in zr_steps[half]:
                        dve.wait_ge(zs_sb, count(k, NZ, 2 * half + 2))
                        g0 = 2 * ZQ * half
                        for s in zr_steps[half][i]:
                            for r in range(4):
                                got = v.tensor_copy(zr[32 * r:32 * r + 32, :, QUADS * s + g0:QUADS * s + g0 + 2 * ZQ],
                                                    zs[32 * s:32 * s + 32, QG * r:QG * (r + 1), g0:g0 + 2 * ZQ])
                        if s == 3:
                            got.then_inc(zr_sb, 1)
                if i == norm_u:
                    dve.wait_ge(u_std, count(k, 1, 1))
                    v.reciprocal(urs[:], usd[:]).then_inc(u_rs, 1)
                for m in range(NBANK):
                    if i == bank_step[m]:
                        dve.wait_ge(t_done, count(k, NBANK, m + 1))
                        v.scalar_tensor_tensor(out=t1[:, m], in0=pT[m % 2][:].rearrange("p (a b) -> p a b", b=PJ),
                                               scalar=col["gs"], in1=bias[:].unsqueeze(1).to_broadcast([P, SBANK, PJ]),
                                               op0=ALU.mult, op1=ALU.add).then_inc(t1_sb, 1)

            n = [0]

            def then(ins):
                n[0] += 1
                ins.then_inc(setup, 1)
                dve.wait_ge(setup, n[0])

            def columns():
                dve.wait_ge(ld_cols, 16)
                dve.wait_ge(bias_done, 1)
                v.tensor_scalar(bias[:], pZ[:, 0:PJ], col["bs"], None, ALU.mult).then_inc(bias_sb, 1)
                for q in range(QG):
                    got = v.tensor_scalar(beye[:, q, :], eye, col["bq"][:, q:q + 1], None, ALU.mult)
                got.then_inc(beye_ready, 1)
                v.tensor_scalar(gg[:], col["gq"], col["gp"], 0.5, ALU.mult, ALU.mult)
                v.tensor_scalar(bp64[:], col["bp"], float(E) / 2, None, ALU.mult)
                v.memset(T[:, :, PJ + 1], 1.0)
                v.memset(w9[:], 0.0)
                v.memset(z9[96:97, :], 1.0)

            def dense():
                dve.wait_ge(x_done, 1)
                for b in range(NBLK):
                    got = v.bn_stats(xstat[:, b, :], pU[:, E * b:E * (b + 1)])
                then(got)
                for b in range(NBLK):
                    got = v.bn_aggr(xmv[:, b, :], xstat[:, b, :])
                got.then_inc(x_var, 1)
                dve.wait_ge(x_std, 1)
                then(v.reciprocal(xrs[:], xsd[:]))
                for b in range(NBLK):
                    got = v.tensor_scalar(xn[:, b, :], pU[:, E * b:E * (b + 1)], xmv[:, b, 0:1], xrs[:, b:b + 1],
                                          ALU.subtract, ALU.mult)
                got.then_inc(x_norm, 1)

            def wl_rows(q):
                dve.wait_ge(wlm_sum, q + 1)
                then(v.tensor_scalar(wlm[:, 1, q:q + 1], wlm[:, 0, q:q + 1], 1.0 / UO, None, ALU.mult))
                v.tensor_scalar(wg[:, q, :], wl_sb[:, q, :], wlm[:, 1, q:q + 1], gg[:, q:q + 1],
                                ALU.subtract, ALU.mult).then_inc(w_ready, 1)

            def s_rows():
                dve.wait_ge(wb_done, 1)
                v.tensor_copy(wbraw[32:64, :], pU[32:64, :]).then_inc(wb_sb, 1)
                v.tensor_scalar(w9[32:64, :], pU[32:64, :], col["gp"][32:64, :], None, ALU.mult)
                dve.wait_ge(ld_wlx, 16)
                v.tensor_scalar(w9[0:32, :], wlx_sb[:], col["gp"][0:32, :], None, ALU.mult)

            def single_rows():
                dve.wait_ge(wrow_done, 1)
                v.tensor_copy(w9[64:65, :], pU[64:65, :])
                then(v.tensor_copy(w9[96:97, :], pU[96:97, :]))
                then(v.tensor_reduce(out=w9m[:, 0:1], in_=w9[:], op=ALU.add, axis=AX.X))
                then(v.tensor_scalar(w9m[:, 1:2], w9m[:, 0:1], 1.0 / UO, None, ALU.mult))
                v.tensor_scalar(w9c[:], w9[:], w9m[:, 1:2], None, ALU.subtract).then_inc(w9_ready, 1)

            v.memset(eps[:], EPS)
            v.memset(ones[:], 1.0).then_inc(fills_ready, 1)
            v.memset(wsc[:], 0.0)
            dve.wait_ge(ld_index, 16)
            v.tensor_tensor(idx[:], idx_in[:, 0, :], idx_in[:, 1, :], ALU.add).then_inc(idx_ready, 1)
            dve.wait_ge(ld_ws, 16)
            then(v.tensor_reduce(out=wsm[:, 0:1], in_=ws_sb[:], op=ALU.add, axis=AX.X))
            then(v.tensor_scalar(wsm[:, 1:2], wsm[:, 0:1], 1.0 / E, None, ALU.mult))
            v.tensor_scalar(wsc[0:D, 0:E], ws_sb[0:D, :], wsm[0:D, 1:2], None, ALU.subtract)
            v.tensor_scalar(wsc[D:P, E:], ws_sb[D:P, :], wsm[D:P, 1:2], None, ALU.subtract).then_inc(wsc_ready, 1)
            dve.wait_ge(ld_wsi, 16)
            then(v.tensor_reduce(out=wsim[:, 0, :], in_=wsi_sb[:], op=ALU.add, axis=AX.X))
            then(v.tensor_scalar(wsim[:, 1, :], wsim[:, 0, :], 1.0 / PJ, None, ALU.mult))
            then(v.tensor_tensor(wsic[:], wsi_sb[:], wsim[:, 1, :].unsqueeze(2).to_broadcast([P, TW, PJ]), ALU.subtract))
            v.memset(z9[:], 0.0).then_inc(wsic_ready, 1)
            dve.wait_ge(ld_const, 16)
            for c in range(TW):
                got = v.tensor_tensor(wexp[:, c], wsic[:, c, :].unsqueeze(1).to_broadcast([P, SPAN, PJ]),
                                      mask[:, c, :].unsqueeze(2).to_broadcast([P, SPAN, PJ]), ALU.mult)
            got.then_inc(wexp_ready, 1)
            run(dve, step, {0: columns, NBLK + 1: dense, S_ROWS: s_rows, S_ROWS + 3: single_rows,
                            **{WL_STEP + 1 + q: functools.partial(wl_rows, q) for q in range(QG)}})


def layout(inputs):
    a = {k: np.asarray(v) for k, v in inputs.items()}
    tables = np.concatenate([a[f"tbl_{f}"] for f in range(NF)], axis=0)
    first_row = np.concatenate([[0], np.cumsum(VOCAB)[:-1]]).astype(np.int32)
    r = np.arange(P * NC)
    t, n = r // NF, r % NF
    sample = (t % 4) * QUADS + t // 4
    ids = a["ids"].reshape(NBLK, P, NF)[:, sample, n].reshape(NBLK, NC, P).transpose(2, 0, 1).reshape(P, NBLK * NC)
    offs = np.broadcast_to(first_row[n].reshape(NC, P).T[:, None, :], (P, NBLK, NC)).reshape(P, NBLK * NC)
    index = np.stack([ids, offs], axis=1).astype(np.int32)
    mask = np.zeros((P, TW, SPAN), np.float32)
    for c in range(TW):
        for p in range(P):
            mask[p, c, (P * c + p) // NF - chunk_samples(c)[0]] = 1.0
    eye = np.tile(np.eye(PJ, dtype=np.float32), (4, 1))
    consts = np.concatenate([np.eye(P, dtype=np.float32), mask.reshape(P, -1), eye], axis=1)
    gsi, bsi = a["L0_rec_gsi"], a["L0_rec_bsi"]
    parts = {
        "bq": np.repeat(bsi.reshape(4, QG), PJ, axis=0), "gq": np.repeat(gsi.reshape(4, QG), PJ, axis=0),
        "bp": np.tile(bsi, 4)[:, None], "gp": np.tile(gsi, 4)[:, None],
        "gs": a["L0_rec_gs"][:, None], "bs": a["L0_rec_bs"][:, None],
        "gd": a["L0_rec_gd"][:, None], "bd": a["L0_rec_bd"][:, None],
        "gl": a["L0_rec_gl"][:USED].reshape(-1, P).T, "bl": a["L0_rec_bl"][:USED].reshape(-1, P).T,
        "b1": a["b_top1"].reshape(-1, P).T, "b2": a["b_top2"].reshape(-1, P).T,
        "w3": a["W_top3"].reshape(-1, P).T,
    }
    small = np.concatenate([parts[name] for name, _ in COLS], axis=1)
    ws_t = np.tile(a["L0_rec_Ws"].T, (2, 1))
    wsi_rows = a["L0_rec_Wsi"].T[n[:P * TW].reshape(TW, P).T]
    dense_t = a["r_dense_t"].T.reshape(DENSE // P, P, B).transpose(1, 0, 2)
    wd_t = a["L0_rec_Wd"].T.reshape(DENSE // P, P, E).transpose(1, 0, 2)
    pair = np.full((PJ, PJ), PJ * (PJ + 1) // 2)
    for p in range(PJ):
        for q in range(p):
            pair[p, q] = pair[q, p] = (p + 1) * p // 2 + q + 1
    wl_t = np.concatenate([a["L0_rec_Wl"].T, np.zeros((1, UO), np.float32)], axis=0)
    wl = wl_t[pair.reshape(PJ, 4, QG).transpose(1, 0, 2)].reshape(P, QG, UO)
    wlx = wl_t[[(p + 1) * p // 2 for p in range(PJ)]]
    return {"tables": tables, "index": index, "consts": consts, "small": small, "ws_t": ws_t, "wsi_rows": wsi_rows,
            "dense_t": dense_t, "wd_t": wd_t, "wl": wl, "wlx": wlx, "w1": a["W_top1"], "w2": a["W_top2"]}


def kernel(**inputs):
    import concourse.bacc as bacc
    from concourse.bass_utils import run_bass_kernel_spmd

    nc = bacc.Bacc("TRN2", target_bir_lowering=False, num_devices=1)
    arrays, args = {}, []
    for name, a in layout(inputs).items():
        a = np.ascontiguousarray(a)
        arrays[f"in_{name}"] = a
        args.append(nc.dram_tensor(f"in_{name}", a.shape, mybir.dt.from_np(a.dtype), kind="ExternalInput").ap())
    out = nc.dram_tensor("out_y", (B, 1), mybir.dt.float32, kind="ExternalOutput").ap()
    build(nc, *args, out.rearrange("b a -> a b"))
    return run_bass_kernel_spmd(nc, [arrays], core_ids=[0]).results[0]["out_y"]
```
